# Optimizing a Trainium2 kernel written in Bass

```python
import numpy as np
import jax
import jax.numpy as jnp

def _softmax(x, axis=-1):
    return jax.nn.softmax(x, axis=axis)

def _gelu(x):
    return jax.nn.gelu(x, approximate=True)

def _silu(x):
    return jax.nn.silu(x)

def _sigmoid(x):
    return jax.nn.sigmoid(x)

def _layernorm(x, axis=-1, eps=1e-05):
    m = jnp.mean(x, axis=axis, keepdims=True)
    v = jnp.var(x, axis=axis, keepdims=True)
    return (x - m) / jnp.sqrt(v + eps)

def _scatter_add(tgt, idx, src, axis=0):
    return tgt.at[idx].add(src)

def _segment_sum(src, seg, n):
    return jax.ops.segment_sum(src, seg, n)
kernel_name = 'mk_cond_seq_d1_seqx_r8_1440aa'

def setup_inputs(seed: int=0):
    np.random.seed(seed)
    _w = jnp.asarray

    def _rec_inputs():
        import jax
        import jax.numpy as jnp
        _rk = jax.random.key(seed)
        x = -0.0003929 + 0.9999 * jax.random.normal(jax.random.fold_in(_rk, 1), (16, 128, 256), jnp.float32)
        _lenS = 128 - jax.random.randint(jax.random.fold_in(_rk, 7), (16,), 0, max(1, 128 // 4) + 1, jnp.int32)
        _lenS2 = 128 - jax.random.randint(jax.random.fold_in(_rk, 8), (16,), 0, max(1, 128 // 4) + 1, jnp.int32)
        pos_BxS = jnp.broadcast_to(jnp.arange(128, dtype=jnp.int32), (16, 128))
        cond_2048 = 0.00782532 + 1.00527 * jax.random.normal(jax.random.fold_in(_rk, 12), (16, 256), jnp.float32)
        return (x, pos_BxS, cond_2048)
    x, pos_BxS, cond_2048 = _rec_inputs()

    def _L0_cond_setup():
        import jax, jax.numpy as jnp
        import numpy as np
        HIDDEN, NQ, NKV, HD, INTER = (256, 8, 1, 32, 1024)
        B, S = (4, 256)
        EPS = 1e-06
        ROPE_BASE = 10000.0

        def ada_rms(x, t, w, tw):
            n = x * jax.lax.rsqrt(jnp.mean(jnp.square(x), axis=-1, keepdims=True) + EPS)
            scale = t @ tw.T
            return n * (w * (1.0 + scale))[:, None, :]

        def apply_rope(x, pos_ids):
            half = HD // 2
            inv_freq = 1.0 / ROPE_BASE ** (jnp.arange(0, HD, 2, dtype=jnp.float32) / HD)
            ang = pos_ids.astype(jnp.float32)[:, :, None] * inv_freq
            cos = jnp.concatenate([jnp.cos(ang), jnp.cos(ang)], axis=-1)[:, None]
            sin = jnp.concatenate([jnp.sin(ang), jnp.sin(ang)], axis=-1)[:, None]
            x1, x2 = (x[..., :half], x[..., half:])
            rot = jnp.concatenate([-x2, x1], axis=-1)
            return x * cos + rot * sin
        key = jax.random.key(seed)
        ks = jax.random.split(key, 12)
        f32 = jnp.float32
        inp = {'x': jax.random.normal(ks[0], (B, S, HIDDEN), f32), 'pos_ids': jnp.broadcast_to(jnp.arange(S, dtype=jnp.int32), (B, S)), 'time_emb': jax.random.normal(ks[1], (B, HIDDEN), f32), 'ln1_w': jnp.ones((HIDDEN,), f32), 'ln1_tw': jax.random.normal(ks[2], (HIDDEN, HIDDEN), f32) * 0.02, 'ln2_w': jnp.ones((HIDDEN,), f32), 'ln2_tw': jax.random.normal(ks[3], (HIDDEN, HIDDEN), f32) * 0.02, 'Wq': jax.random.normal(ks[4], (NQ * HD, HIDDEN), f32) * 0.02, 'Wk': jax.random.normal(ks[5], (NKV * HD, HIDDEN), f32) * 0.02, 'Wv': jax.random.normal(ks[6], (NKV * HD, HIDDEN), f32) * 0.02, 'Wo': jax.random.normal(ks[7], (HIDDEN, NQ * HD), f32) * 0.02, 'Wg': jax.random.normal(ks[8], (INTER, HIDDEN), f32) * 0.02, 'Wu': jax.random.normal(ks[9], (INTER, HIDDEN), f32) * 0.02, 'Wd': jax.random.normal(ks[10], (HIDDEN, INTER), f32) * 0.02}
        return inp
    _L0_cond_all = _L0_cond_setup()
    _L0_cond_in = {k: v for k, v in _L0_cond_all.items() if k in ('ln1_w', 'ln1_tw', 'ln2_w', 'ln2_tw', 'Wq', 'Wk', 'Wv', 'Wo', 'Wg', 'Wu', 'Wd')}
    del _L0_cond_all
    return {'x': x, 'pos_BxS': pos_BxS, 'cond_2048': cond_2048, 'L0_cond_ln1_w': _L0_cond_in['ln1_w'], 'L0_cond_ln1_tw': _L0_cond_in['ln1_tw'], 'L0_cond_ln2_w': _L0_cond_in['ln2_w'], 'L0_cond_ln2_tw': _L0_cond_in['ln2_tw'], 'L0_cond_Wq': _L0_cond_in['Wq'], 'L0_cond_Wk': _L0_cond_in['Wk'], 'L0_cond_Wv': _L0_cond_in['Wv'], 'L0_cond_Wo': _L0_cond_in['Wo'], 'L0_cond_Wg': _L0_cond_in['Wg'], 'L0_cond_Wu': _L0_cond_in['Wu'], 'L0_cond_Wd': _L0_cond_in['Wd']}

def reference(x, pos_BxS, cond_2048, L0_cond_ln1_w, L0_cond_ln1_tw, L0_cond_ln2_w, L0_cond_ln2_tw, L0_cond_Wq, L0_cond_Wk, L0_cond_Wv, L0_cond_Wo, L0_cond_Wg, L0_cond_Wu, L0_cond_Wd):
    import jax
    import jax.numpy as jnp

    def _L0_cond_ref(x, pos_ids, time_emb, ln1_w, ln1_tw, ln2_w, ln2_tw, Wq, Wk, Wv, Wo, Wg, Wu, Wd):
        import jax, jax.numpy as jnp
        import numpy as np
        HIDDEN, NQ, NKV, HD, INTER = (256, 8, 1, 32, 1024)
        B, S = (4, 256)
        EPS = 1e-06
        ROPE_BASE = 10000.0

        def ada_rms(x, t, w, tw):
            n = x * jax.lax.rsqrt(jnp.mean(jnp.square(x), axis=-1, keepdims=True) + EPS)
            scale = t @ tw.T
            return n * (w * (1.0 + scale))[:, None, :]

        def apply_rope(x, pos_ids):
            half = HD // 2
            inv_freq = 1.0 / ROPE_BASE ** (jnp.arange(0, HD, 2, dtype=jnp.float32) / HD)
            ang = pos_ids.astype(jnp.float32)[:, :, None] * inv_freq
            cos = jnp.concatenate([jnp.cos(ang), jnp.cos(ang)], axis=-1)[:, None]
            sin = jnp.concatenate([jnp.sin(ang), jnp.sin(ang)], axis=-1)[:, None]
            x1, x2 = (x[..., :half], x[..., half:])
            rot = jnp.concatenate([-x2, x1], axis=-1)
            return x * cos + rot * sin
        b, s, _ = x.shape
        g = NQ // NKV
        res = x
        h = ada_rms(x, time_emb, ln1_w, ln1_tw)
        q = (h @ Wq.T).reshape(b, s, NQ, HD).transpose(0, 2, 1, 3)
        k = (h @ Wk.T).reshape(b, s, NKV, HD).transpose(0, 2, 1, 3)
        v = (h @ Wv.T).reshape(b, s, NKV, HD).transpose(0, 2, 1, 3)
        q = apply_rope(q, pos_ids)
        k = apply_rope(k, pos_ids)
        qg = q.reshape(b, NKV, g, s, HD)
        scores = jnp.einsum('bkgsd,bktd->bkgst', qg, k) / jnp.sqrt(jnp.float32(HD))
        attn = jax.nn.softmax(scores, axis=-1)
        ctx = jnp.einsum('bkgst,bktd->bkgsd', attn, v)
        ctx = ctx.reshape(b, NQ, s, HD).transpose(0, 2, 1, 3).reshape(b, s, NQ * HD)
        x = res + ctx @ Wo.T
        res = x
        h = ada_rms(x, time_emb, ln2_w, ln2_tw)
        mlp = jax.nn.silu(h @ Wg.T) * (h @ Wu.T) @ Wd.T
        return res + mlp
    x = _L0_cond_ref(x, pos_BxS, cond_2048, L0_cond_ln1_w, L0_cond_ln1_tw, L0_cond_ln2_w, L0_cond_ln2_tw, L0_cond_Wq, L0_cond_Wk, L0_cond_Wv, L0_cond_Wo, L0_cond_Wg, L0_cond_Wu, L0_cond_Wd)
    return x

_drawn_inputs = setup_inputs


def setup_inputs(seed=0):
    import zlib

    import numpy as np

    out = dict(_drawn_inputs(seed))
    spreads = {'L0_cond_ln1_w': (1.0, 0.6), 'L0_cond_ln2_w': (1.0, 0.6)}
    factors = {'cond_2048': 3.204,
     'L0_cond_ln1_tw': 8.0,
     'L0_cond_ln2_tw': 3.131,
     'L0_cond_Wq': 8.0,
     'L0_cond_Wk': 8.0,
     'L0_cond_Wv': 5.724,
     'L0_cond_Wo': 5.722,
     'L0_cond_Wg': 2.803}
    for name, (base, spread) in spreads.items():
        noise = np.random.default_rng([zlib.crc32(name.encode()), seed]).standard_normal(out[name].shape)
        drawn = base * np.exp(spread * noise) if base else spread * noise
        out[name] = jnp.asarray(drawn.astype(out[name].dtype))
    for name, factor in factors.items():
        out[name] = (out[name] * factor).astype(out[name].dtype)
    return out
```

```python
from contextlib import ExitStack

import numpy as np

import concourse.bass as bass
from concourse import mybir
from concourse.alu_op_type import AluOpType as ALU

ACT = mybir.ActivationFunctionType
AX = mybir.AxisListType
F32, F32R, I32 = mybir.dt.float32, mybir.dt.float32r, mybir.dt.int32
F16, BF16 = mybir.dt.float16, mybir.dt.bfloat16

P = 128
B, S, HID = 16, 128, 256
NQ, HD, INTER = 8, 32, 1024
HALF = HD // 2
EPS = 1e-6
ROPE_BASE = 10000.0
C = HID // P
QKV = (NQ + 2) * HD
G = B // 2
TOK = 2 * S
J = INTER // P
NPAIR = J // 2
HH = NQ // 2
VW = 3 * HD + 1
SCALE = float(HD) ** -0.5
LOG_P = 12 * float(np.log(2.0))
TWO_PI = 2 * np.pi
PI_A = 6.28125
PI_B = float(np.round((TWO_PI - PI_A) * 2.0**20) / 2.0**20)
PI_C = float(np.float32(TWO_PI - PI_A - PI_B))
TRIG_STEPS = 12
ROUND = 1.5 * 2.0**23
PI_MAX = float(np.nextafter(np.float32(np.pi), np.float32(0)))


def layer_kernel(nc, x, xT, pos, inv_freq, ident, condT, tw, ln_w, wqkv, wo, wgu, wd, out):
    with ExitStack() as ctx:
        def sb(name, shape, dt=F32):
            return ctx.enter_context(nc.sbuf_tensor(name, shape, dt))

        def bank(name):
            return ctx.enter_context(nc.psum_tensor(name, [P, 512], F32))

        def sem(name):
            return ctx.enter_context(nc.semaphore(name))

        bank_a = bank("bank_a")
        bank_b = bank("bank_b")
        half_ps = [bank("half0_ps"), bank("half1_ps")]
        mlp_ps = ctx.enter_context(nc.psum_tensor("mlp_ps", [P, 4, 2, TOK], F32))

        ident_sb = sb("ident_sb", [P, P])
        pos_sb, pos_f = sb("pos_sb", [P, B], I32), sb("pos_f", [P, B])
        freq_sb = sb("freq_sb", [P, HALF])
        cond_sb = sb("cond_sb", [P, C, B])
        tw_sb = sb("tw_sb", [P, 2, C, HID])
        lnw_sb = sb("lnw_sb", [P, 2, C])
        wqkv_sb, wqkv_hi, wqkv_lo = sb("wqkv_sb", [P, C, QKV]), sb("wqkv_hi", [P, C, QKV], F32R), sb("wqkv_lo", [P, C, QKV], F32R)
        wo_sb, wo_hi, wo_lo = sb("wo_sb", [P, C, HID]), sb("wo_hi", [P, C, HID], F32R), sb("wo_lo", [P, C, HID], F32R)
        wgu_sb, wgu_hi, wgu_lo = sb("wgu_sb", [P, C, 2, INTER]), sb("wgu_hi", [P, C, 2, INTER], F32R), sb("wgu_lo", [P, C, 2, INTER], F32R)
        wd_sb, wd_hi, wd_lo = sb("wd_sb", [P, J, HID]), sb("wd_hi", [P, J, HID], F32R), sb("wd_lo", [P, J, HID], F32R)
        ada = sb("ada", [P, 2, C, B])
        cos_t, sin_t = sb("cos_t", [P, B, HD]), sb("sin_t", [P, B, HD])
        ang, turns, angle = sb("ang", [P, B, HALF]), sb("turns", [P, 2, B, HALF]), sb("angle", [P, 2, B, HALF])
        minus_half, eps, zeros = sb("minus_half", [P, 2]), sb("eps", [P, 2]), sb("zeros", [P, HD])

        x_sb = sb("x_sb", [P, B, HID])
        xT_sb = sb("xT_sb", [P, B, C, S])
        junk = sb("junk", [P, HID])
        ms1, var1, rstd1 = sb("ms1", [P, 2]), sb("var1", [P, 2]), sb("rstd1", [P, 2])
        ms2, var2, rstd2 = sb("ms2", [P, 2]), sb("var2", [P, 2]), sb("rstd2", [P, 2])
        h_hi, h_lo = sb("h_hi", [P, 2, C, S], F32R), sb("h_lo", [P, 2, C, S], F32R)
        qkv = sb("qkv", [P, NQ + 2, HD])
        rope_c, rope_s, roped = sb("rope_c", [P, NQ + 1, HD]), sb("rope_s", [P, NQ + 1, HD]), sb("roped", [P, NQ + 1, HD])
        q_hl = sb("q_hl", [P, NQ, 2, HD], F32R)
        k_hl = sb("k_hl", [P, 2, 4, HD], F32R)
        q_st = sb("q_st", [P, NQ // 2, S], F32R)
        k_bd = sb("k_bd", [P, 2, 2, S], F32R)
        v_parts, v_rest = sb("v_parts", [P, VW], BF16), sb("v_rest", [P, HD])
        smax, shift = sb("smax", [P, NQ]), sb("shift", [P, NQ])
        probs = sb("probs", [P, NQ, S])
        pT_hi, pT_lo = sb("pT_hi", [P, NQ, S], F16), sb("pT_lo", [P, NQ, S], F16)
        ctx_sum, rden, ctx_n = sb("ctx_sum", [P, NQ, HD]), sb("rden", [P, NQ]), sb("ctx_n", [P, NQ, HD])
        cT_hi, cT_lo = sb("cT_hi", [P, C, S], F32R), sb("cT_lo", [P, C, S], F32R)
        x2n = sb("x2n", [P, 2, HID])
        h2_hi, h2_lo = sb("h2_hi", [P, C, TOK], F32R), sb("h2_lo", [P, C, TOK], F32R)
        th, sg, act_m = sb("th", [P, 2, TOK]), sb("sg", [P, 2, TOK]), sb("act_m", [P, 2, TOK])
        m_hi, m_lo = sb("m_hi", [P, J, TOK], F32R), sb("m_lo", [P, J, TOK], F32R)

        ld_xT, ld_x, ld_cond, ld_wqkv, ld_rope, ld_ident = (
            sem(n) for n in ("ld_xT", "ld_x", "ld_cond", "ld_wqkv", "ld_rope", "ld_ident"))
        ld_wo, ld_wgu, ld_wd, stored = sem("ld_wo"), sem("ld_wgu"), sem("ld_wd"), sem("stored")
        ada_mm, ada_done, consts_set, zeros_set, ones_set, trig_step, table_done = (
            sem(n) for n in ("ada_mm", "ada_done", "consts_set", "zeros_set", "ones_set", "trig_step", "table_done"))
        qkv_w_hi, qkv_w_lo, o_w_hi, o_w_lo, mlp_w_hi, mlp_w_lo = (
            sem(n) for n in ("qkv_w_hi", "qkv_w_lo", "o_w_hi", "o_w_lo", "mlp_w_hi", "mlp_w_lo"))
        sq_step, sq1_done, var1_done, rstd1_done, h_hi_done, h_lo_done = (
            sem(n) for n in ("sq_step", "sq1_done", "var1_done", "rstd1_done", "h_hi_done", "h_lo_done"))
        qkv_mm, qkv_done, rope_step, v_step, v_done, q_hi_done, q_lo_done, k_hi_done, k_lo_done = (
            sem(n) for n in ("qkv_mm", "qkv_done", "rope_step", "v_step", "v_done", "q_hi_done", "q_lo_done", "k_hi_done", "k_lo_done"))
        k_turned, q_turned, k_ready, q_ready = (sem(n) for n in ("k_turned", "q_turned", "k_ready", "q_ready"))
        scores_mm, max_done, shift_done, exp_done, p_turned, p_hi_done, p_lo_done = (
            sem(n) for n in ("scores_mm", "max_done", "shift_done", "exp_done", "p_turned", "p_hi_done", "p_lo_done"))
        ctx_mm, ctx_summed, rden_done, ctx_done = (sem(n) for n in ("ctx_mm", "ctx_summed", "rden_done", "ctx_done"))
        c_turned, c_hi_done, c_lo_done, wo_mm, x2_done, sq2_done, var2_done, rstd2_done = (
            sem(n) for n in ("c_turned", "c_hi_done", "c_lo_done", "wo_mm", "x2_done", "sq2_done", "var2_done", "rstd2_done"))
        x2n_done, x2_turned, h2_hi_done, h2_lo_done = (sem(n) for n in ("x2n_done", "x2_turned", "h2_hi_done", "h2_lo_done"))
        gu_mm, tanh_done = sem("gu_mm"), sem("tanh_done")
        primed = gate_done, m_done, m_hi_done, m_lo_done, down_mm, y_done = [
            sem(n) for n in ("gate_done", "m_done", "m_hi_done", "m_lo_done", "down_mm", "y_done")]

        block = ctx.enter_context(nc.Block())

        def wait(engine, semaphore, count):
            if semaphore in primed:
                engine.wait_ge(semaphore, count + 1)
            elif not (isinstance(count, int) and count <= 0):
                engine.wait_ge(semaphore, count)

        def pick(t):
            return bass.ds(t, 1)

        def schedule(engine, part):
            part(0, None, True)
            with engine.Fori(1, G - 1) as g:
                part(g, g - 1, True)
            part(G - 1, G - 2, False)
            part(None, G - 1, False)

        @block.sync
        def _(sp):
            def load_group(g):
                sp.dma_start(xT_sb[:, bass.ds(2 * g, 2)], xT[:, bass.ds(2 * g, 2)]).then_inc(ld_xT, 16)
                sp.dma_start(x_sb[:, bass.ds(2 * g, 2)], x[:, bass.ds(2 * g, 2)]).then_inc(ld_x, 16)

            sp.dma_start(cond_sb[:], condT).then_inc(ld_cond, 16)
            sp.dma_start(tw_sb[:], tw).then_inc(ld_cond, 16)
            load_group(0)
            sp.dma_start(ident_sb[:], ident).then_inc(ld_ident, 16)
            sp.dma_start(wgu_sb[:], wgu).then_inc(ld_wgu, 16)
            sp.dma_start(wd_sb[:], wd).then_inc(ld_wd, 16)
            with sp.Fori(1, G) as g:
                sp.wait_ge(ld_xT, 16 * g)
                sp.wait_ge(ld_x, 16 * g)
                load_group(g)
            with sp.Fori(0, G) as g:
                wait(sp, y_done, 2 * g + 2)
                sp.dma_start(out[:, bass.ds(2 * g, 2)], x_sb[:, bass.ds(2 * g, 2)]).then_inc(stored, 16)
            sp.wait_ge(stored, 16 * G)

        @block.gpsimd
        def _(pool):
            for s in primed:
                pool.sem_inc(s, 1)
            nc.gpsimd.memset(k_bd[:].bitcast(F32), 0.0).then_inc(zeros_set, 1)
            nc.gpsimd.memset(v_parts[:], 1.0).then_inc(ones_set, 1)

            def rstd1_of(g):
                wait(pool, sq1_done, g + 1)
                wait(pool, qkv_done, 2 * g)
                nc.gpsimd.tensor_tensor(var1[:], ms1[:], eps[:], ALU.add).then_inc(var1_done, 1)
                wait(pool, var1_done, g + 1)
                nc.gpsimd.tensor_tensor(rstd1[:], var1[:], minus_half[:], ALU.pow).then_inc(rstd1_done, 1)

            def split_v(t):
                v = qkv[:, NQ + 1, :]
                wait(pool, qkv_done, t + 1)
                wait(pool, ctx_mm, 2 * t)
                nc.gpsimd.tensor_tensor(v_parts[:, 0:HD], v, zeros[:], ALU.add).then_inc(v_step, 1)
                wait(pool, v_step, 3 * t + 1)
                nc.gpsimd.tensor_tensor(v_rest[:], v, v_parts[:, 0:HD], ALU.subtract).then_inc(v_step, 1)
                wait(pool, v_step, 3 * t + 2)
                nc.gpsimd.tensor_tensor(v_parts[:, HD:2 * HD], v_rest[:], zeros[:], ALU.add).then_inc(v_step, 1)
                wait(pool, v_step, 3 * t + 3)
                nc.gpsimd.tensor_tensor(v_parts[:, 2 * HD:3 * HD], v_rest[:], v_parts[:, HD:2 * HD],
                                        ALU.subtract).then_inc(v_done, 1)

            def rstd2_of(t, s):
                wait(pool, sq2_done, t + 1)
                wait(pool, x2n_done, t - 1)
                nc.gpsimd.tensor_tensor(var2[:, s:s + 1], ms2[:, s:s + 1], eps[:, 0:1], ALU.add).then_inc(var2_done, 1)
                wait(pool, var2_done, t + 1)
                nc.gpsimd.tensor_tensor(rstd2[:, s:s + 1], var2[:, s:s + 1], minus_half[:, 0:1],
                                        ALU.pow).then_inc(rstd2_done, 1)

            def low_of_pair(m, q):
                wait(pool, m_hi_done, NPAIR * m + q + 1)
                nc.gpsimd.tensor_tensor(m_lo[:, 2 * q:2 * q + 2], act_m[:], m_hi[:, 2 * q:2 * q + 2].bitcast(F32),
                                        ALU.subtract).then_inc(m_lo_done, 1)

            def part(g, m, more):
                if g is None:
                    for q in range(NPAIR):
                        low_of_pair(m, q)
                    return
                for s in range(2):
                    t = 2 * g + s
                    split_v(t)
                    if m is not None:
                        for q in ((0, 1), (3,))[s]:
                            low_of_pair(m, q)
                    if s == 1 and more:
                        rstd1_of(g + 1)
                    rstd2_of(t, s)
                    if m is not None and s == 0:
                        low_of_pair(m, 2)
                    if m is None and s == 0:
                        pool.wait_ge(mlp_w_hi, 2)
                        for c in range(C):
                            nc.gpsimd.tensor_tensor(wgu_lo[:, c], wgu_sb[:, c], wgu_hi[:, c].bitcast(F32),
                                                    ALU.subtract).then_inc(mlp_w_lo, 1)

            pool.wait_ge(consts_set, 3)
            rstd1_of(0)
            schedule(pool, part)

        @block.scalar
        def _(act):
            act.dma_start(wqkv_sb[:], wqkv).then_inc(ld_wqkv, 16)
            act.dma_start(lnw_sb[:], ln_w).then_inc(ld_cond, 16)
            act.dma_start(pos_sb[:], pos).then_inc(ld_rope, 16)
            act.dma_start(freq_sb[:], inv_freq).then_inc(ld_rope, 16)
            act.dma_start(wo_sb[:], wo).then_inc(ld_wo, 16)

            def norm1_prep(g):
                wait(act, ld_x, 16 * (g + 1))
                for s in range(2):
                    wait(act, sq2_done, 2 * g - 1)
                    if s:
                        wait(act, sq_step, g + 1)
                    sq = nc.scalar.activation(junk[:], x_sb[:, pick(2 * g + s)], ACT.Square, scale=HID ** -0.5,
                                              accum_out=ms1[:, s:s + 1])
                    sq.then_inc(sq1_done if s else sq_step, 1)
                wait(act, ld_xT, 16 * (g + 1))
                wait(act, ada_done, 1)
                for s in range(2):
                    for c in range(C):
                        hi = nc.scalar.activation(h_hi[:, s, c], xT_sb[:, pick(2 * g + s), c], ACT.Copy,
                                                  scale=ada[:, 0, c, pick(2 * g + s)])
                hi.then_inc(h_hi_done, 1)

            def tanh_of_pair(m, q):
                wait(act, gu_mm, NPAIR * m + q + 1)
                wait(act, gate_done, NPAIR * m + q)
                k = 2 * (q % 2)
                nc.scalar.activation(th[:], mlp_ps[:, k:k + 2, 0], ACT.Tanh, scale=0.5).then_inc(tanh_done, 1)

            def high_of_pair(m, q):
                wait(act, m_done, NPAIR * m + q + 1)
                wait(act, down_mm, 2 * m)
                nc.scalar.activation(m_hi[:, 2 * q:2 * q + 2], act_m[:], ACT.Copy).then_inc(m_hi_done, 1)

            def norm2_high(g, s):
                t = 2 * g + s
                wait(act, x2_turned, t + 1)
                for c in range(C):
                    hi = nc.scalar.activation(h2_hi[:, c, s * S:(s + 1) * S], bank_b[:, c * S:(c + 1) * S], ACT.Copy,
                                              scale=ada[:, 1, c, pick(t)])
                hi.then_inc(h2_hi_done, 1)

            def part(g, m, more):
                if g is None:
                    for q in range(NPAIR):
                        tanh_of_pair(m, q)
                        high_of_pair(m, q)
                    return
                for s in range(2):
                    t = 2 * g + s
                    wait(act, qkv_mm, t + 1)
                    wait(act, rstd1_done, g + 1)
                    wait(act, rope_step, 3 * t)
                    wait(act, v_done, t)
                    nc.scalar.activation(qkv[:], bank_a[:, 0:QKV].rearrange("p (h d) -> p h d", d=HD), ACT.Copy,
                                         scale=rstd1[:, s:s + 1]).then_inc(qkv_done, 1)
                    wait(act, rope_step, 3 * t + 3)
                    wait(act, q_turned, t)
                    nc.scalar.activation(q_hl[:, :, 0], roped[:, 0:NQ], ACT.Copy).then_inc(q_hi_done, 1)
                    if m is not None:
                        q = 3 * s
                        tanh_of_pair(m, q)
                        high_of_pair(m, q)
                    if s == 1:
                        norm2_high(g, 0)
                    wait(act, k_turned, t + 1)
                    wait(act, scores_mm, 2 * t)
                    if isinstance(t, int) and t == 0:
                        act.wait_ge(zeros_set, 1)
                    for i in range(2):
                        rows = slice(64 * i, 64 * i + 64)
                        k = nc.scalar.activation(k_bd[rows, :, i], bank_a[rows, 0:2 * S].rearrange("p (l t) -> p l t", l=2),
                                                 ACT.Copy)
                    k.then_inc(k_ready, 1)
                    wait(act, q_turned, t + 1)
                    nc.scalar.activation(q_st[:], bank_b[:].rearrange("p (h t) -> p h t", t=S), ACT.Copy).then_inc(q_ready, 1)
                    if s == 1 and more:
                        norm1_prep(g + 1)
                    if m is None and s == 1:
                        for c in range(J // 4):
                            nc.scalar.activation(wd_hi[:, 4 * c:4 * c + 4], wd_sb[:, 4 * c:4 * c + 4], ACT.Copy).then_inc(mlp_w_hi, 1)
                    for i in range(2):
                        wait(act, shift_done, 2 * t + i + 1)
                        wait(act, p_turned, 2 * (t - 1) + i + 1)
                        for h in range(HH):
                            e = nc.scalar.activation(probs[:, HH * i + h], half_ps[i][:, h * S:(h + 1) * S], ACT.Exp,
                                                     scale=SCALE, bias=shift[:, HH * i + h:HH * i + h + 1])
                        e.then_inc(exp_done, 1)
                    if m is not None and s == 0:
                        tanh_of_pair(m, 1)
                    for i in range(2):
                        wait(act, p_turned, 2 * t + i + 1)
                        wait(act, ctx_mm, 2 * (t - 1) + i + 1)
                        nc.scalar.activation(pT_hi[:, HH * i:HH * i + HH], (bank_b, bank_a)[i][:].rearrange("p (h t) -> p h t", t=S),
                                             ACT.Copy).then_inc(p_hi_done, 1)
                    if m is not None and s == 0:
                        high_of_pair(m, 1)
                    if m is None and s == 0:
                        act.wait_ge(ld_wgu, 16)
                        for c in range(C):
                            nc.scalar.activation(wgu_hi[:, c], wgu_sb[:, c], ACT.Copy).then_inc(mlp_w_hi, 1)
                        act.wait_ge(ld_wd, 16)
                    wait(act, c_turned, t + 1)
                    wait(act, wo_mm, t)
                    nc.scalar.activation(cT_hi[:], bank_b[:, 0:HID].rearrange("p (c t) -> p c t", t=S), ACT.Copy).then_inc(c_hi_done, 1)
                    wait(act, x2_done, t + 1)
                    wait(act, sq2_done, t)
                    wait(act, sq1_done, g + 1 if not (s == 1 and more) else g + 2)
                    wait(act, rstd2_done, t - 1)
                    nc.scalar.activation(junk[:], x_sb[:, pick(t)], ACT.Square, scale=HID ** -0.5,
                                         accum_out=ms2[:, s:s + 1]).then_inc(sq2_done, 1)
                    if m is not None and s == 0:
                        tanh_of_pair(m, 2)
                        high_of_pair(m, 2)
                    if s == 1:
                        norm2_high(g, 1)

            act.wait_ge(ld_wqkv, 16)
            nc.scalar.activation(wqkv_hi[:], wqkv_sb[:], ACT.Copy).then_inc(qkv_w_hi, 1)
            norm1_prep(0)
            act.wait_ge(ld_wo, 16)
            nc.scalar.activation(wo_hi[:], wo_sb[:], ACT.Copy).then_inc(o_w_hi, 1)
            act.wait_ge(trig_step, TRIG_STEPS)
            for i, sign in ((0, -1.0), (1, 1.0)):
                nc.scalar.activation(sin_t[:, :, i * HALF:(i + 1) * HALF], angle[:, 0], ACT.Sin, scale=sign)
                table = nc.scalar.activation(cos_t[:, :, i * HALF:(i + 1) * HALF], angle[:, 1], ACT.Sin)
            table.then_inc(table_done, 1)
            schedule(act, part)

        @block.tensor
        def _(pe):
            def three_passes(out_ap, a_hi, a_lo, b_hi, b_lo, first, last):
                nc.tensor.matmul(out_ap, a_hi, b_hi, start=first, stop=False)
                nc.tensor.matmul(out_ap, a_hi, b_lo, start=False, stop=False)
                return nc.tensor.matmul(out_ap, a_lo, b_hi, start=False, stop=last)

            def mlp_piece(m, i):
                if i < 2 * J:
                    j, which = divmod(i, 2)
                    q = j // 2
                    if i == 0:
                        wait(pe, h2_hi_done, 2 * m + 2)
                        wait(pe, h2_lo_done, 2 * m + 2)
                        wait(pe, y_done, 2 * m)
                    elif i % 4 == 0:
                        wait(pe, m_done, NPAIR * m + q - 1)
                    ps = mlp_ps[:, 2 * (q % 2) + j % 2, which]
                    for c in range(C):
                        cols = slice(j * P, (j + 1) * P)
                        mm = three_passes(ps, wgu_hi[:, c, which, cols], wgu_lo[:, c, which, cols],
                                          h2_hi[:, c], h2_lo[:, c], c == 0, c == C - 1)
                    if i % 4 == 3:
                        mm.then_inc(gu_mm, 1)
                else:
                    s, k = divmod(i - 2 * J, 4)
                    if s == 0:
                        if k == 0:
                            wait(pe, m_done, NPAIR * m + 3)
                        wait(pe, m_lo_done, NPAIR * m + k + 1)
                    for j in (2 * k, 2 * k + 1):
                        tokens = slice(s * S, (s + 1) * S)
                        mm = three_passes(mlp_ps[:, s, 0], m_hi[:, j, tokens], m_lo[:, j, tokens],
                                          wd_hi[:, j], wd_lo[:, j], j == 0, j == J - 1)
                    if k == 3:
                        mm.then_inc(down_mm, 1)

            def turn_x2(g, s):
                wait(pe, x2n_done, 2 * g + s + 1)
                for c in range(C):
                    mm = nc.tensor.transpose(bank_b[:, c * S:(c + 1) * S], x2n[:, s, c * P:(c + 1) * P], ident_sb[:])
                mm.then_inc(x2_turned, 1)

            def part(g, m, more):
                if m is None:
                    pieces = iter(())
                else:
                    pieces = iter(range(24))

                def mlp(n):
                    for _ in range(n):
                        i = next(pieces, None)
                        if i is not None:
                            mlp_piece(m, i)

                if g is None:
                    mlp(24)
                    return
                for s in range(2):
                    t = 2 * g + s
                    wait(pe, h_hi_done, g + 1)
                    wait(pe, h_lo_done, g + 1)
                    wait(pe, x2_done, t)
                    for c in range(C):
                        mm = three_passes(bank_a[:, 0:QKV], h_hi[:, s, c], h_lo[:, s, c], wqkv_hi[:, c], wqkv_lo[:, c],
                                          c == 0, c == C - 1)
                    mm.then_inc(qkv_mm, 1)
                    mlp(4)
                    if s == 1:
                        turn_x2(g, 0)
                    wait(pe, k_lo_done, t + 1)
                    for i in range(2):
                        mm = nc.tensor.transpose(bank_a[:, i * S:(i + 1) * S],
                                                 k_hl[:, i].rearrange("p r d -> p (r d)").bitcast(F32), ident_sb[:])
                    mm.then_inc(k_turned, 1)
                    wait(pe, q_lo_done, t + 1)
                    wait(pe, h2_hi_done, t)
                    wait(pe, h2_lo_done, t)
                    for i in range(NQ // 2):
                        mm = nc.tensor.transpose(bank_b[:, i * S:(i + 1) * S],
                                                 q_hl[:, 2 * i:2 * i + 2].rearrange("p h l d -> p (h l d)").bitcast(F32),
                                                 ident_sb[:])
                    mm.then_inc(q_turned, 1)
                    mlp(1)
                    wait(pe, k_ready, t + 1)
                    wait(pe, q_ready, t + 1)
                    for i in range(2):
                        wait(pe, ctx_done, 2 * (t - 1) + i + 1)
                        for a in range(2):
                            for l in range(2):
                                mm = nc.tensor.matmul(half_ps[i][:, a * 2 * S:(a + 1) * 2 * S], q_st[:, 2 * i + a],
                                                      k_bd[:, l].rearrange("p h t -> p (h t)"), start=(l == 0), stop=(l == 1))
                        mm.then_inc(scores_mm, 1)
                    mlp(3)
                    for i in range(2):
                        wait(pe, exp_done, 2 * t + i + 1)
                        for h in range(HH):
                            mm = nc.tensor.transpose((bank_b, bank_a)[i][:, h * S:(h + 1) * S], probs[:, HH * i + h], ident_sb[:])
                        mm.then_inc(p_turned, 1)
                    mlp(1)
                    wait(pe, v_done, t + 1)
                    for i in range(2):
                        wait(pe, p_hi_done, 2 * t + i + 1)
                        wait(pe, p_lo_done, 2 * t + i + 1)
                        for h in range(HH):
                            for k, part_of_p in enumerate((pT_hi, pT_lo)):
                                mm = nc.tensor.matmul(half_ps[i][:, h * VW:(h + 1) * VW], part_of_p[:, HH * i + h], v_parts[:],
                                                      start=(k == 0), stop=(k == 1))
                        mm.then_inc(ctx_mm, 1)
                    mlp(1)
                    wait(pe, ctx_done, 2 * t + 2)
                    for c in range(C):
                        mm = nc.tensor.transpose(bank_b[:, c * S:(c + 1) * S],
                                                 ctx_n[:, HH * c:HH * c + HH].rearrange("p h d -> p (h d)"), ident_sb[:])
                    mm.then_inc(c_turned, 1)
                    mlp(1)
                    wait(pe, c_hi_done, t + 1)
                    wait(pe, c_lo_done, t + 1)
                    if isinstance(t, int) and t == 0:
                        pe.wait_ge(o_w_hi, 1)
                        pe.wait_ge(o_w_lo, 1)
                    for c in range(C):
                        mm = three_passes(bank_a[:, 0:HID], cT_hi[:, c], cT_lo[:, c], wo_hi[:, c], wo_lo[:, c], c == 0, c == C - 1)
                    mm.then_inc(wo_mm, 1)
                    mlp(1)
                turn_x2(g, 1)
                if m is None:
                    pe.wait_ge(mlp_w_lo, 4)

            pe.wait_ge(ld_cond, 48)
            for n in range(2):
                for c in range(C):
                    for k in range(C):
                        mm = nc.tensor.matmul(half_ps[0][:, (C * n + c) * B:(C * n + c + 1) * B], tw_sb[:, n, k, c * P:(c + 1) * P],
                                              cond_sb[:, k], start=(k == 0), stop=(k == C - 1))
            mm.then_inc(ada_mm, 1)
            pe.wait_ge(qkv_w_hi, 1)
            pe.wait_ge(qkv_w_lo, 1)
            pe.wait_ge(ld_ident, 16)
            schedule(pe, part)

        @block.vector
        def _(dve):
            def norm1_low(g):
                wait(dve, h_hi_done, g + 1)
                for s in range(2):
                    for c in range(C):
                        lo = nc.vector.scalar_tensor_tensor(h_lo[:, s, c], xT_sb[:, pick(2 * g + s), c].rearrange("p o t -> p (o t)"),
                                                            ada[:, 0, c, pick(2 * g + s)], h_hi[:, s, c].bitcast(F32),
                                                            ALU.mult, ALU.subtract)
                lo.then_inc(h_lo_done, 1)

            def gate_pair(m, q):
                k = 2 * (q % 2)
                wait(dve, tanh_done, NPAIR * m + q + 1)
                wait(dve, m_done, NPAIR * m + q)
                nc.vector.scalar_tensor_tensor(sg[:], th[:], 1.0, mlp_ps[:, k:k + 2, 0], ALU.add, ALU.mult).then_inc(gate_done, 1)
                wait(dve, gate_done, NPAIR * m + q + 1)
                wait(dve, m_lo_done, NPAIR * m + q)
                nc.vector.scalar_tensor_tensor(act_m[:], sg[:], 0.5, mlp_ps[:, k:k + 2, 1], ALU.mult, ALU.mult).then_inc(m_done, 1)

            def norm2_low(g, s):
                t = 2 * g + s
                wait(dve, h2_hi_done, t + 1)
                for c in range(C):
                    tokens = slice(s * S, (s + 1) * S)
                    lo = nc.vector.scalar_tensor_tensor(h2_lo[:, c, tokens], bank_b[:, c * S:(c + 1) * S], ada[:, 1, c, pick(t)],
                                                        h2_hi[:, c, tokens].bitcast(F32), ALU.mult, ALU.subtract)
                lo.then_inc(h2_lo_done, 1)

            def finish(m, s):
                t = 2 * m + s
                wait(dve, down_mm, t + 1)
                nc.vector.tensor_tensor(x_sb[:, pick(t)], x_sb[:, pick(t)], mlp_ps[:, s, 0].unsqueeze(1), ALU.add).then_inc(y_done, 1)

            def part(g, m, more):
                if g is None:
                    for q in range(NPAIR):
                        gate_pair(m, q)
                    finish(m, 0)
                    finish(m, 1)
                    return
                for s in range(2):
                    t = 2 * g + s
                    heads = [P, NQ + 1, HD]
                    wait(dve, qkv_done, t + 1)
                    nc.vector.tensor_tensor(rope_c[:], qkv[:, 0:NQ + 1], cos_t[:, pick(t)].broadcast_to(heads), ALU.mult).then_inc(rope_step, 1)
                    for i in range(2):
                        here, there = slice(i * HALF, (i + 1) * HALF), slice((1 - i) * HALF, (2 - i) * HALF)
                        sw = nc.vector.tensor_tensor(rope_s[:, :, here], qkv[:, 0:NQ + 1, there],
                                                     sin_t[:, pick(t), here].broadcast_to([P, NQ + 1, HALF]), ALU.mult)
                    sw.then_inc(rope_step, 1)
                    wait(dve, rope_step, 3 * t + 2)
                    wait(dve, q_hi_done, t)
                    nc.vector.tensor_tensor(roped[:], rope_c[:], rope_s[:], ALU.add).then_inc(rope_step, 1)
                    wait(dve, rope_step, 3 * t + 3)
                    wait(dve, k_turned, t)
                    k4 = roped[:, NQ:NQ + 1].broadcast_to([P, 4, HD])
                    nc.vector.tensor_copy(k_hl[:, 0], k4).then_inc(k_hi_done, 1)
                    wait(dve, k_hi_done, t + 1)
                    nc.vector.tensor_tensor(k_hl[:, 1], k4, k_hl[:, 0].bitcast(F32), ALU.subtract).then_inc(k_lo_done, 1)
                    wait(dve, q_hi_done, t + 1)
                    nc.vector.tensor_tensor(q_hl[:, :, 1], roped[:, 0:NQ], q_hl[:, :, 0].bitcast(F32), ALU.subtract).then_inc(q_lo_done, 1)
                    if m is not None:
                        gate_pair(m, 3 * s)
                    if s == 1:
                        norm2_low(g, 0)
                    for i in range(2):
                        half = slice(HH * i, HH * i + HH)
                        wait(dve, scores_mm, 2 * t + i + 1)
                        wait(dve, exp_done, 2 * (t - 1) + i + 1)
                        nc.vector.tensor_reduce(smax[:, half], half_ps[i][:].rearrange("p (h t) -> p h t", t=S), AX.X,
                                                ALU.max).then_inc(max_done, 1)
                        wait(dve, max_done, 2 * t + i + 1)
                        nc.vector.tensor_scalar(shift[:, half], smax[:, half], -SCALE, LOG_P, ALU.mult, ALU.add).then_inc(shift_done, 1)
                    if m is not None:
                        if s == 0:
                            gate_pair(m, 1)
                        else:
                            finish(m, 0)
                    if s == 1 and more:
                        norm1_low(g + 1)
                    for i in range(2):
                        half = slice(HH * i, HH * i + HH)
                        wait(dve, p_hi_done, 2 * t + i + 1)
                        nc.vector.tensor_tensor(pT_lo[:, half], (bank_b, bank_a)[i][:].rearrange("p (h t) -> p h t", t=S), pT_hi[:, half],
                                                ALU.subtract).then_inc(p_lo_done, 1)
                    if m is None and s == 0:
                        dve.wait_ge(ld_wo, 16)
                        dve.wait_ge(o_w_hi, 1)
                        nc.vector.tensor_tensor(wo_lo[:], wo_sb[:], wo_hi[:].bitcast(F32), ALU.subtract).then_inc(o_w_lo, 1)
                    for i in range(2):
                        half = slice(HH * i, HH * i + HH)
                        heads_ps = half_ps[i][:, 0:HH * VW].rearrange("p (h w) -> p h w", w=VW)
                        wait(dve, ctx_mm, 2 * t + i + 1)
                        wait(dve, c_turned, t)
                        nc.vector.reciprocal(rden[:, half].unsqueeze(2), heads_ps[:, :, 3 * HD:VW]).then_inc(rden_done, 1)
                        nc.vector.tensor_reduce(ctx_sum[:, half], heads_ps[:, :, 0:3 * HD].rearrange("p h (k d) -> p h d k", k=3), AX.X,
                                                ALU.add).then_inc(ctx_summed, 1)
                        wait(dve, rden_done, 2 * t + i + 1)
                        wait(dve, ctx_summed, 2 * t + i + 1)
                        nc.vector.tensor_tensor(ctx_n[:, half], ctx_sum[:, half], rden[:, half].unsqueeze(2).broadcast_to([P, HH, HD]),
                                                ALU.mult).then_inc(ctx_done, 1)
                    wait(dve, c_hi_done, t + 1)
                    nc.vector.tensor_tensor(cT_lo[:], bank_b[:, 0:HID].rearrange("p (c t) -> p c t", t=S), cT_hi[:].bitcast(F32),
                                            ALU.subtract).then_inc(c_lo_done, 1)
                    wait(dve, wo_mm, t + 1)
                    nc.vector.tensor_tensor(x_sb[:, pick(t)], x_sb[:, pick(t)], bank_a[:, 0:HID].unsqueeze(1), ALU.add).then_inc(x2_done, 1)
                    if m is None and s == 1:
                        dve.wait_ge(mlp_w_hi, 4)
                        for c in range(2):
                            nc.vector.tensor_tensor(wd_lo[:, 4 * c:4 * c + 4], wd_sb[:, 4 * c:4 * c + 4], wd_hi[:, 4 * c:4 * c + 4].bitcast(F32),
                                                    ALU.subtract).then_inc(mlp_w_lo, 1)
                    wait(dve, x2_done, t + 1)
                    wait(dve, rstd2_done, t + 1)
                    wait(dve, x2_turned, t - 1)
                    nc.vector.tensor_scalar(x2n[:, s:s + 1], x_sb[:, pick(t)], rstd2[:, s:s + 1], None, ALU.mult).then_inc(x2n_done, 1)
                    if m is not None:
                        if s == 0:
                            gate_pair(m, 2)
                        else:
                            finish(m, 1)
                norm2_low(g, 1)

            nc.vector.memset(minus_half[:], -0.5).then_inc(consts_set, 1)
            nc.vector.memset(eps[:], EPS).then_inc(consts_set, 1)
            nc.vector.memset(zeros[:], 0.0).then_inc(consts_set, 1)
            dve.wait_ge(ld_wqkv, 16)
            dve.wait_ge(qkv_w_hi, 1)
            nc.vector.tensor_tensor(wqkv_lo[:], wqkv_sb[:], wqkv_hi[:].bitcast(F32), ALU.subtract).then_inc(qkv_w_lo, 1)
            dve.wait_ge(ada_mm, 1)
            dve.wait_ge(ld_cond, 48)
            for n in range(2):
                for c in range(C):
                    a = nc.vector.tensor_scalar(ada[:, n, c], half_ps[0][:, (C * n + c) * B:(C * n + c + 1) * B], 1.0,
                                                lnw_sb[:, n, c:c + 1], ALU.add, ALU.mult)
            a.then_inc(ada_done, 1)
            dve.wait_ge(ada_done, 1)
            norm1_low(0)
            steps = [0]

            def trig(ins):
                steps[0] += 1
                ins.then_inc(trig_step, 1)
                dve.wait_ge(trig_step, steps[0])

            dve.wait_ge(ld_rope, 32)
            trig(nc.vector.tensor_copy(pos_f[:], pos_sb[:]))
            trig(nc.vector.tensor_tensor(ang[:], pos_f[:].unsqueeze(2).broadcast_to([P, B, HALF]),
                                         freq_sb[:].unsqueeze(1).broadcast_to([P, B, HALF]), ALU.mult))
            trig(nc.vector.tensor_scalar(turns[:, 0], ang[:], 1 / TWO_PI, None, ALU.mult))
            trig(nc.vector.tensor_scalar(turns[:, 1], ang[:], 1 / TWO_PI, 0.25, ALU.mult, ALU.add))
            trig(nc.vector.tensor_scalar(turns[:], turns[:], ROUND, ROUND, ALU.add, ALU.subtract))
            trig(nc.vector.tensor_copy(angle[:, 0], ang[:]))
            trig(nc.vector.tensor_copy(angle[:, 1], ang[:]))
            for piece in (PI_A, PI_B, PI_C):
                trig(nc.vector.scalar_tensor_tensor(angle[:], turns[:], -piece, angle[:], ALU.mult, ALU.add))
            trig(nc.vector.tensor_scalar(angle[:, 1], angle[:, 1], np.pi / 2, None, ALU.add))
            trig(nc.vector.tensor_scalar(angle[:], angle[:], PI_MAX, -PI_MAX, ALU.min, ALU.max))
            assert steps[0] == TRIG_STEPS
            dve.wait_ge(table_done, 1)
            schedule(dve, part)


def kernel(x, pos_BxS, cond_2048, L0_cond_ln1_w, L0_cond_ln1_tw, L0_cond_ln2_w, L0_cond_ln2_tw, L0_cond_Wq, L0_cond_Wk,
           L0_cond_Wv, L0_cond_Wo, L0_cond_Wg, L0_cond_Wu, L0_cond_Wd):
    import concourse.bacc as _bacc
    from concourse.bass_utils import run_bass_kernel_spmd as _run

    def rows(a):
        a = np.asarray(a)
        return np.ascontiguousarray(np.moveaxis(a.reshape(-1, P, *a.shape[1:]), 0, 1))

    x = np.asarray(x)
    freq = (1.0 / ROPE_BASE ** (np.arange(0, HD, 2, dtype=np.float32) / HD)).astype(np.float32)
    arrays = {
        "x": np.ascontiguousarray(x.transpose(1, 0, 2)),
        "xT": np.ascontiguousarray(x.reshape(B, S, C, P).transpose(3, 0, 2, 1)),
        "pos": np.ascontiguousarray(np.asarray(pos_BxS).T),
        "inv_freq": np.tile(freq, (P, 1)),
        "ident": np.eye(P, dtype=np.float32),
        "condT": rows(np.asarray(cond_2048).T),
        "tw": np.ascontiguousarray(np.stack([rows(np.asarray(w).T) for w in (L0_cond_ln1_tw, L0_cond_ln2_tw)], 1)),
        "ln_w": np.ascontiguousarray(np.stack([rows(w) for w in (L0_cond_ln1_w, L0_cond_ln2_w)], 1)),
        "wqkv": rows(np.concatenate([np.asarray(w) for w in (L0_cond_Wq, L0_cond_Wk, L0_cond_Wv)]).T),
        "wo": rows(np.asarray(L0_cond_Wo).T),
        "wgu": rows(np.stack([np.asarray(w).T for w in (L0_cond_Wg, L0_cond_Wu)], 1)),
        "wd": rows(np.asarray(L0_cond_Wd).T),
    }
    nc = _bacc.Bacc("TRN2", target_bir_lowering=False, num_devices=1)
    args = [nc.dram_tensor(f"in_{n}_dram", a.shape, mybir.dt.from_np(a.dtype), kind="ExternalInput").ap() for n, a in arrays.items()]
    out = nc.dram_tensor("out_dram", (S, B, HID), F32, kind="ExternalOutput").ap()
    layer_kernel(nc, *args, out)
    r = _run(nc, [{f"in_{n}_dram": a for n, a in arrays.items()}], core_ids=[0])
    return np.ascontiguousarray(r.results[0]["out_dram"].transpose(1, 0, 2))
```

```python
from contextlib import ExitStack

import numpy as np

import concourse.bass as bass
from concourse import mybir
from concourse.alu_op_type import AluOpType as ALU

ACT = mybir.ActivationFunctionType
AX = mybir.AxisListType
F32, F32R, I32 = mybir.dt.float32, mybir.dt.float32r, mybir.dt.int32
F16, BF16 = mybir.dt.float16, mybir.dt.bfloat16

P = 128
B, S, HID = 16, 128, 256
NQ, HD, INTER = 8, 32, 1024
HALF = HD // 2
EPS = 1e-6
ROPE_BASE = 10000.0
C = HID // P
QKV = (NQ + 2) * HD
G = B // 2
TOK = 2 * S
J = INTER // P
NPAIR = J // 2
HH = NQ // 2
VW = 3 * HD + 1
SCALE = float(HD) ** -0.5
LOG_P = 12 * float(np.log(2.0))
TWO_PI = 2 * np.pi
PI_A = 6.28125
PI_B = float(np.round((TWO_PI - PI_A) * 2.0**20) / 2.0**20)
PI_C = float(np.float32(TWO_PI - PI_A - PI_B))
TRIG_STEPS = 12
ROUND = 1.5 * 2.0**23
PI_MAX = float(np.nextafter(np.float32(np.pi), np.float32(0)))


def layer_kernel(nc, x, xT, pos, inv_freq, ident, condT, tw, ln_w, wqkv, wo, wgu, wd, out):
    with ExitStack() as ctx:
        def sb(name, shape, dt=F32):
            return ctx.enter_context(nc.sbuf_tensor(name, shape, dt))

        def bank(name):
            return ctx.enter_context(nc.psum_tensor(name, [P, 512], F32))

        def sem(name):
            return ctx.enter_context(nc.semaphore(name))

        bank_a = bank("bank_a")
        bank_b = bank("bank_b")
        half_ps = [bank("half0_ps"), bank("half1_ps")]
        mlp_ps = ctx.enter_context(nc.psum_tensor("mlp_ps", [P, 4, 2, TOK], F32))

        ident_sb = sb("ident_sb", [P, P])
        pos_sb, pos_f = sb("pos_sb", [P, B], I32), sb("pos_f", [P, B])
        freq_sb = sb("freq_sb", [P, HALF])
        cond_sb = sb("cond_sb", [P, C, B])
        tw_sb = sb("tw_sb", [P, 2, C, HID])
        lnw_sb = sb("lnw_sb", [P, 2, C])
        wqkv_sb, wqkv_hi, wqkv_lo = sb("wqkv_sb", [P, C, QKV]), sb("wqkv_hi", [P, C, QKV], F32R), sb("wqkv_lo", [P, C, QKV], F32R)
        wo_sb, wo_hi, wo_lo = sb("wo_sb", [P, C, HID]), sb("wo_hi", [P, C, HID], F32R), sb("wo_lo", [P, C, HID], F32R)
        wgu_sb, wgu_hi, wgu_lo = sb("wgu_sb", [P, C, 2, INTER]), sb("wgu_hi", [P, C, 2, INTER], F32R), sb("wgu_lo", [P, C, 2, INTER], F32R)
        wd_sb, wd_hi, wd_lo = sb("wd_sb", [P, J, HID]), sb("wd_hi", [P, J, HID], F32R), sb("wd_lo", [P, J, HID], F32R)
        ada = sb("ada", [P, 2, C, B])
        cos_t, sin_t = sb("cos_t", [P, B, HD]), sb("sin_t", [P, B, HD])
        ang, turns, angle = sb("ang", [P, B, HALF]), sb("turns", [P, 2, B, HALF]), sb("angle", [P, 2, B, HALF])
        minus_half, eps, zeros = sb("minus_half", [P, 1]), sb("eps", [P, 1]), sb("zeros", [P, HD])

        x_sb = sb("x_sb", [P, B, HID])
        xT_sb = sb("xT_sb", [P, B, C, S])
        junk1, junk2 = sb("junk1", [P, HID]), sb("junk2", [P, HID])
        ms1, var1, rstd1 = sb("ms1", [P, 2]), sb("var1", [P, 2]), sb("rstd1", [P, 2])
        ms2, var2, rstd2 = sb("ms2", [P, 2]), sb("var2", [P, 2]), sb("rstd2", [P, 2])
        h_hi, h_lo = sb("h_hi", [P, 2, C, S], F32R), sb("h_lo", [P, 2, C, S], F32R)
        qkv = sb("qkv", [P, NQ + 2, HD])
        rope_c, rope_s, roped = sb("rope_c", [P, NQ + 1, HD]), sb("rope_s", [P, NQ + 1, HD]), sb("roped", [P, NQ + 1, HD])
        q_hl = sb("q_hl", [P, NQ, 2, HD], F32R)
        k_hl = sb("k_hl", [P, 2, 4, HD], F32R)
        q_st = sb("q_st", [P, NQ // 2, S], F32R)
        k_bd = sb("k_bd", [P, 2, 2, S], F32R)
        v_parts, v_rest = sb("v_parts", [P, VW], BF16), sb("v_rest", [P, HD])
        smax, shift = sb("smax", [P, NQ]), sb("shift", [P, NQ])
        probs = sb("probs", [P, NQ, S])
        pT_hi, pT_lo = sb("pT_hi", [P, NQ, S], F16), sb("pT_lo", [P, NQ, S], F16)
        ctx_sum, rden, ctx_n = sb("ctx_sum", [P, NQ, HD]), sb("rden", [P, NQ]), sb("ctx_n", [P, NQ, HD])
        cT_hi, cT_lo = sb("cT_hi", [P, C, S], F32R), sb("cT_lo", [P, C, S], F32R)
        x2n = sb("x2n", [P, 2, HID])
        h2_hi, h2_lo = sb("h2_hi", [P, C, TOK], F32R), sb("h2_lo", [P, C, TOK], F32R)
        th, sg, act_m = sb("th", [P, 2, TOK]), sb("sg", [P, 2, TOK]), sb("act_m", [P, 2, TOK])
        m_hi, m_lo = sb("m_hi", [P, J, TOK], F32R), sb("m_lo", [P, J, TOK], F32R)

        ld_xT, ld_x, ld_cond, ld_wqkv, ld_rope, ld_ident = (
            sem(n) for n in ("ld_xT", "ld_x", "ld_cond", "ld_wqkv", "ld_rope", "ld_ident"))
        ld_wo, ld_wgu, ld_wd, stored = sem("ld_wo"), sem("ld_wgu"), sem("ld_wd"), sem("stored")
        ada_mm, ada_done, consts_set, zeros_set, ones_set, trig_step, table_done = (
            sem(n) for n in ("ada_mm", "ada_done", "consts_set", "zeros_set", "ones_set", "trig_step", "table_done"))
        qkv_w_hi, qkv_w_lo, o_w_hi, o_w_lo, mlp_w_hi, mlp_w_lo = (
            sem(n) for n in ("qkv_w_hi", "qkv_w_lo", "o_w_hi", "o_w_lo", "mlp_w_hi", "mlp_w_lo"))
        sq1_done, var1_done, rstd1_done, h_hi_done, h_lo_done = (
            sem(n) for n in ("sq1_done", "var1_done", "rstd1_done", "h_hi_done", "h_lo_done"))
        qkv_mm, qkv_done, rope_step, v_step, v_done, q_hi_done, q_lo_done, k_hi_done, k_lo_done = (
            sem(n) for n in ("qkv_mm", "qkv_done", "rope_step", "v_step", "v_done", "q_hi_done", "q_lo_done", "k_hi_done", "k_lo_done"))
        k_turned, q_turned, k_ready, q_ready = (sem(n) for n in ("k_turned", "q_turned", "k_ready", "q_ready"))
        scores_mm, max_done, shift_done, exp_done, p_turned, p_hi_done, p_lo_done = (
            sem(n) for n in ("scores_mm", "max_done", "shift_done", "exp_done", "p_turned", "p_hi_done", "p_lo_done"))
        ctx_mm, ctx_summed, rden_done, ctx_done = (sem(n) for n in ("ctx_mm", "ctx_summed", "rden_done", "ctx_done"))
        c_turned, c_hi_done, c_lo_done, wo_mm, x2_done, sq2_done, var2_done, rstd2_done = (
            sem(n) for n in ("c_turned", "c_hi_done", "c_lo_done", "wo_mm", "x2_done", "sq2_done", "var2_done", "rstd2_done"))
        x2n_done, x2_turned, h2_hi_done, h2_lo_done = (sem(n) for n in ("x2n_done", "x2_turned", "h2_hi_done", "h2_lo_done"))
        gu_mm, tanh_done = sem("gu_mm"), sem("tanh_done")
        primed = gate_done, m_done, m_hi_done, m_lo_done, down_mm, y_done = [
            sem(n) for n in ("gate_done", "m_done", "m_hi_done", "m_lo_done", "down_mm", "y_done")]

        block = ctx.enter_context(nc.Block())

        def wait(engine, semaphore, count):
            if semaphore in primed:
                engine.wait_ge(semaphore, count + 1)
            elif not (isinstance(count, int) and count <= 0):
                engine.wait_ge(semaphore, count)

        def pick(t):
            return bass.ds(t, 1)

        def schedule(engine, part):
            part(0, None, True)
            with engine.Fori(1, G - 1) as g:
                part(g, g - 1, True)
            part(G - 1, G - 2, False)
            part(None, G - 1, False)


        @block.sync
        def _(sp):
            def load_group(g):
                sp.dma_start(xT_sb[:, bass.ds(2 * g, 2)], xT[:, bass.ds(2 * g, 2)]).then_inc(ld_xT, 16)
                sp.dma_start(x_sb[:, bass.ds(2 * g, 2)], x[:, bass.ds(2 * g, 2)]).then_inc(ld_x, 16)

            sp.dma_start(cond_sb[:], condT).then_inc(ld_cond, 16)
            sp.dma_start(tw_sb[:], tw).then_inc(ld_cond, 16)
            load_group(0)
            sp.dma_start(ident_sb[:], ident).then_inc(ld_ident, 16)
            sp.wait_ge(ld_xT, 16)
            sp.wait_ge(ld_x, 16)
            load_group(1)
            sp.dma_start(wgu_sb[:], wgu).then_inc(ld_wgu, 16)
            sp.dma_start(wd_sb[:], wd).then_inc(ld_wd, 16)
            with sp.Fori(2, G) as g:
                sp.wait_ge(ld_xT, 16 * g)
                sp.wait_ge(ld_x, 16 * g)
                load_group(g)
            with sp.Fori(0, G) as g:
                wait(sp, y_done, 2 * g + 2)
                sp.dma_start(out[:, bass.ds(2 * g, 2)], x_sb[:, bass.ds(2 * g, 2)]).then_inc(stored, 16)
            sp.wait_ge(stored, 16 * G)

        @block.gpsimd
        def _(pool):
            for s in primed:
                pool.sem_inc(s, 1)
            nc.gpsimd.memset(k_bd[:].bitcast(F32), 0.0).then_inc(zeros_set, 1)
            nc.gpsimd.memset(v_parts[:], 1.0).then_inc(ones_set, 1)

            def rstd1_of(t, s):
                wait(pool, sq1_done, t + 1)
                wait(pool, qkv_done, t - 1)
                nc.gpsimd.tensor_tensor(var1[:, s:s + 1], ms1[:, s:s + 1], eps[:], ALU.add).then_inc(var1_done, 1)
                wait(pool, var1_done, t + 1)
                nc.gpsimd.tensor_tensor(rstd1[:, s:s + 1], var1[:, s:s + 1], minus_half[:], ALU.pow).then_inc(rstd1_done, 1)

            def split_v(t):
                v = qkv[:, NQ + 1, :]
                wait(pool, qkv_done, t + 1)
                wait(pool, ctx_mm, 2 * t)
                nc.gpsimd.tensor_tensor(v_parts[:, 0:HD], v, zeros[:], ALU.add).then_inc(v_step, 1)
                wait(pool, v_step, 3 * t + 1)
                nc.gpsimd.tensor_tensor(v_rest[:], v, v_parts[:, 0:HD], ALU.subtract).then_inc(v_step, 1)
                wait(pool, v_step, 3 * t + 2)
                nc.gpsimd.tensor_tensor(v_parts[:, HD:2 * HD], v_rest[:], zeros[:], ALU.add).then_inc(v_step, 1)
                wait(pool, v_step, 3 * t + 3)
                nc.gpsimd.tensor_tensor(v_parts[:, 2 * HD:3 * HD], v_rest[:], v_parts[:, HD:2 * HD],
                                        ALU.subtract).then_inc(v_done, 1)

            def rope_sum(t):
                wait(pool, rope_step, 3 * t + 2)
                wait(pool, q_hi_done, t)
                wait(pool, k_hi_done, t)
                nc.gpsimd.tensor_tensor(roped[:], rope_c[:], rope_s[:], ALU.add).then_inc(rope_step, 1)

            def qk_low(t):
                wait(pool, q_hi_done, t + 1)
                nc.gpsimd.tensor_tensor(q_hl[:, :, 1], roped[:, 0:NQ], q_hl[:, :, 0].bitcast(F32), ALU.subtract).then_inc(q_lo_done, 1)
                wait(pool, k_hi_done, t + 1)
                nc.gpsimd.tensor_tensor(k_hl[:, 1], roped[:, NQ:NQ + 1].broadcast_to([P, 4, HD]), k_hl[:, 0].bitcast(F32),
                                        ALU.subtract).then_inc(k_lo_done, 1)

            def rstd2_of(t, s):
                wait(pool, sq2_done, t + 1)
                wait(pool, x2n_done, t - 1)
                nc.gpsimd.tensor_tensor(var2[:, s:s + 1], ms2[:, s:s + 1], eps[:], ALU.add).then_inc(var2_done, 1)
                wait(pool, var2_done, t + 1)
                nc.gpsimd.tensor_tensor(rstd2[:, s:s + 1], var2[:, s:s + 1], minus_half[:], ALU.pow).then_inc(rstd2_done, 1)

            def low_of_pair(m, q):
                wait(pool, m_hi_done, NPAIR * m + q + 1)
                nc.gpsimd.tensor_tensor(m_lo[:, 2 * q:2 * q + 2], act_m[:], m_hi[:, 2 * q:2 * q + 2].bitcast(F32),
                                        ALU.subtract).then_inc(m_lo_done, 1)

            def part(g, m, more):
                if g is None:
                    for q in range(NPAIR):
                        low_of_pair(m, q)
                    return
                for s in range(2):
                    t = 2 * g + s
                    if more or s == 0:
                        qk_low(t + 1)
                    if m is not None and s == 1:
                        low_of_pair(m, 2)
                    if more:
                        rstd1_of(t + 2, s)
                    if more or s == 0:
                        split_v(t + 1)
                    rstd2_of(t, s)
                    if more:
                        rope_sum(t + 2)
                    if m is not None:
                        low_of_pair(m, 3 * s)
                    if m is not None and s == 0:
                        low_of_pair(m, 1)
                    if m is None and s == 0:
                        for c in range(C):
                            pool.wait_ge(mlp_w_hi, c + 1)
                            nc.gpsimd.tensor_tensor(wgu_lo[:, c], wgu_sb[:, c], wgu_hi[:, c].bitcast(F32),
                                                    ALU.subtract).then_inc(mlp_w_lo, 1)

            pool.wait_ge(consts_set, 3)
            rstd1_of(0, 0)
            rstd1_of(1, 1)
            rope_sum(0)
            qk_low(0)
            split_v(0)
            rope_sum(1)
            schedule(pool, part)

        @block.scalar
        def _(act):
            act.dma_start(wqkv_sb[:], wqkv).then_inc(ld_wqkv, 16)
            act.dma_start(lnw_sb[:], ln_w).then_inc(ld_cond, 16)
            act.dma_start(pos_sb[:], pos).then_inc(ld_rope, 16)
            act.dma_start(freq_sb[:], inv_freq).then_inc(ld_rope, 16)
            act.dma_start(wo_sb[:], wo).then_inc(ld_wo, 16)

            def norm1_prep(t, s, loaded):
                wait(act, ld_x, 16 * loaded)
                wait(act, sq1_done, t)
                wait(act, rstd1_done, t - 1)
                nc.scalar.activation(junk1[:], x_sb[:, pick(t)], ACT.Square, scale=HID ** -0.5,
                                     accum_out=ms1[:, s:s + 1]).then_inc(sq1_done, 1)
                wait(act, ld_xT, 16 * loaded)
                wait(act, ada_done, 1)
                wait(act, qkv_mm, t - 1)
                for c in range(C):
                    hi = nc.scalar.activation(h_hi[:, s, c], xT_sb[:, pick(t), c], ACT.Copy, scale=ada[:, 0, c, pick(t)])
                hi.then_inc(h_hi_done, 1)

            def qkv_out(t, s):
                wait(act, qkv_mm, t + 1)
                wait(act, rstd1_done, t + 1)
                wait(act, rope_step, 3 * t)
                wait(act, v_done, t)
                nc.scalar.activation(qkv[:], bank_a[:, 0:QKV].rearrange("p (h d) -> p h d", d=HD), ACT.Copy,
                                     scale=rstd1[:, s:s + 1]).then_inc(qkv_done, 1)

            def qk_high(t):
                wait(act, rope_step, 3 * t + 3)
                wait(act, q_turned, t)
                nc.scalar.activation(q_hl[:, :, 0], roped[:, 0:NQ], ACT.Copy).then_inc(q_hi_done, 1)
                wait(act, k_turned, t)
                nc.scalar.activation(k_hl[:, 0], roped[:, NQ:NQ + 1].broadcast_to([P, 4, HD]), ACT.Copy).then_inc(k_hi_done, 1)

            def k_out(t):
                wait(act, k_turned, t + 1)
                wait(act, scores_mm, 2 * t)
                for i in range(2):
                    rows = slice(64 * i, 64 * i + 64)
                    k = nc.scalar.activation(k_bd[rows, :, i], bank_a[rows, 0:2 * S].rearrange("p (l t) -> p l t", l=2), ACT.Copy)
                k.then_inc(k_ready, 1)

            def q_out(t):
                wait(act, q_turned, t + 1)
                nc.scalar.activation(q_st[:], bank_b[:].rearrange("p (h t) -> p h t", t=S), ACT.Copy).then_inc(q_ready, 1)

            def exps(t, i):
                wait(act, shift_done, 2 * t + i + 1)
                wait(act, p_turned, 2 * (t - 1) + i + 1)
                for h in range(HH * i, HH * i + HH):
                    e = nc.scalar.activation(probs[:, h], half_ps[i][:, (h % HH) * S:(h % HH + 1) * S], ACT.Exp,
                                             scale=SCALE, bias=shift[:, h:h + 1])
                e.then_inc(exp_done, 1)

            def p_high(t, i):
                wait(act, p_turned, 2 * t + i + 1)
                wait(act, ctx_mm, 2 * (t - 1) + i + 1)
                nc.scalar.activation(pT_hi[:, HH * i:HH * i + HH], (bank_b, bank_a)[i][:].rearrange("p (h t) -> p h t", t=S),
                                     ACT.Copy).then_inc(p_hi_done, 1)

            def c_high(t):
                wait(act, c_turned, t + 1)
                wait(act, wo_mm, t)
                nc.scalar.activation(cT_hi[:], bank_a[:, 0:HID].rearrange("p (c t) -> p c t", t=S), ACT.Copy).then_inc(c_hi_done, 1)

            def square2(t, s):
                wait(act, x2_done, t + 1)
                wait(act, sq2_done, t)
                wait(act, rstd2_done, t - 1)
                nc.scalar.activation(junk2[:], x_sb[:, pick(t)], ACT.Square, scale=HID ** -0.5,
                                     accum_out=ms2[:, s:s + 1]).then_inc(sq2_done, 1)

            def norm2_high(t, s):
                wait(act, x2_turned, t + 1)
                for c in range(C):
                    hi = nc.scalar.activation(h2_hi[:, c, s * S:(s + 1) * S], mlp_ps[:, 2 * s + 1, 0, c * S:(c + 1) * S], ACT.Copy,
                                              scale=ada[:, 1, c, pick(t)])
                hi.then_inc(h2_hi_done, 1)

            def tanh_of_pair(m, q):
                wait(act, gu_mm, NPAIR * m + q + 1)
                wait(act, gate_done, NPAIR * m + q)
                k = 2 * (q % 2)
                nc.scalar.activation(th[:], mlp_ps[:, k:k + 2, 0], ACT.Tanh, scale=0.5).then_inc(tanh_done, 1)

            def high_of_pair(m, q):
                wait(act, m_done, NPAIR * m + q + 1)
                wait(act, down_mm, 2 * m)
                nc.scalar.activation(m_hi[:, 2 * q:2 * q + 2], act_m[:], ACT.Copy).then_inc(m_hi_done, 1)

            def part(g, m, more):
                if g is None:
                    for q in range(NPAIR):
                        if q:
                            tanh_of_pair(m, q)
                        high_of_pair(m, q)
                    return
                for s in range(2):
                    t = 2 * g + s
                    mid = more or s == 0
                    if mid:
                        qk_high(t + 1)
                    p_high(t, 0)
                    p_high(t, 1)
                    if m is not None and s == 1:
                        tanh_of_pair(m, 2)
                    if more:
                        norm1_prep(t + 2, s, g + 2)
                    if mid:
                        k_out(t + 1)
                        q_out(t + 1)
                    if m is not None and s == 1:
                        high_of_pair(m, 2)
                    if m is None and s == 0:
                        act.wait_ge(ld_wgu, 16)
                        nc.scalar.activation(wgu_hi[:, 0], wgu_sb[:, 0], ACT.Copy).then_inc(mlp_w_hi, 1)
                    c_high(t)
                    if m is not None:
                        tanh_of_pair(m, 3 * s)
                    if s == 1:
                        norm2_high(t - 1, 0)
                    if mid:
                        exps(t + 1, 0)
                    if m is not None:
                        high_of_pair(m, 3 * s)
                    square2(t, s)
                    if more:
                        qkv_out(t + 2, s)
                    if mid:
                        exps(t + 1, 1)
                    if m is not None and s == 0:
                        tanh_of_pair(m, 1)
                        high_of_pair(m, 1)
                    if m is None and s == 0:
                        nc.scalar.activation(wgu_hi[:, 1], wgu_sb[:, 1], ACT.Copy).then_inc(mlp_w_hi, 1)
                    if m is None and s == 1:
                        act.wait_ge(ld_wd, 16)
                        nc.scalar.activation(wd_hi[:], wd_sb[:], ACT.Copy).then_inc(mlp_w_hi, 1)
                    if s == 1:
                        norm2_high(t, 1)
                if not more:
                    tanh_of_pair(m + 1, 0)

            act.wait_ge(ld_wqkv, 16)
            nc.scalar.activation(wqkv_hi[:], wqkv_sb[:], ACT.Copy).then_inc(qkv_w_hi, 1)
            norm1_prep(0, 0, 1)
            norm1_prep(1, 1, 1)
            act.wait_ge(trig_step, TRIG_STEPS)
            for i, sign in ((0, -1.0), (1, 1.0)):
                nc.scalar.activation(sin_t[:, :, i * HALF:(i + 1) * HALF], angle[:, 0], ACT.Sin, scale=sign)
                table = nc.scalar.activation(cos_t[:, :, i * HALF:(i + 1) * HALF], angle[:, 1], ACT.Sin)
            table.then_inc(table_done, 1)
            qkv_out(0, 0)
            act.wait_ge(ld_wo, 16)
            nc.scalar.activation(wo_hi[:], wo_sb[:], ACT.Copy).then_inc(o_w_hi, 1)
            qk_high(0)
            act.wait_ge(zeros_set, 1)
            k_out(0)
            q_out(0)
            exps(0, 0)
            exps(0, 1)
            qkv_out(1, 1)
            schedule(act, part)

        @block.tensor
        def _(pe):
            def three_passes(out_ap, a_hi, a_lo, b_hi, b_lo, first, last):
                nc.tensor.matmul(out_ap, a_hi, b_hi, start=first, stop=False)
                nc.tensor.matmul(out_ap, a_hi, b_lo, start=False, stop=False)
                return nc.tensor.matmul(out_ap, a_lo, b_hi, start=False, stop=last)

            def project_qkv(t, s):
                wait(pe, h_lo_done, t + 1)
                wait(pe, c_lo_done, t - 1)
                for c in range(C):
                    mm = three_passes(bank_a[:, 0:QKV], h_hi[:, s, c], h_lo[:, s, c], wqkv_hi[:, c], wqkv_lo[:, c],
                                      c == 0, c == C - 1)
                mm.then_inc(qkv_mm, 1)

            def turn_qk(t):
                wait(pe, k_lo_done, t + 1)
                wait(pe, p_lo_done, 2 * t)
                for i in range(2):
                    mm = nc.tensor.transpose(bank_a[:, i * S:(i + 1) * S],
                                             k_hl[:, i].rearrange("p r d -> p (r d)").bitcast(F32), ident_sb[:])
                mm.then_inc(k_turned, 1)
                for i in range(NQ // 2):
                    mm = nc.tensor.transpose(bank_b[:, i * S:(i + 1) * S],
                                             q_hl[:, 2 * i:2 * i + 2].rearrange("p h l d -> p (h l d)").bitcast(F32),
                                             ident_sb[:])
                mm.then_inc(q_turned, 1)

            def scores(t):
                wait(pe, k_ready, t + 1)
                wait(pe, q_ready, t + 1)
                for i in range(2):
                    wait(pe, ctx_done, 2 * (t - 1) + i + 1)
                    for a in range(2):
                        for l in range(2):
                            mm = nc.tensor.matmul(half_ps[i][:, a * 2 * S:(a + 1) * 2 * S], q_st[:, 2 * i + a],
                                                  k_bd[:, l].rearrange("p h t -> p (h t)"), start=(l == 0), stop=(l == 1))
                    mm.then_inc(scores_mm, 1)

            def turn_probs(t, last):
                for i in range(2):
                    wait(pe, exp_done, 2 * t + i + 1)
                    if i == 0:
                        wait(pe, x2_done, t)
                    elif not last:
                        wait(pe, qkv_done, t + 2)
                    for h in range(HH):
                        mm = nc.tensor.transpose((bank_b, bank_a)[i][:, h * S:(h + 1) * S], probs[:, HH * i + h], ident_sb[:])
                    mm.then_inc(p_turned, 1)

            def context(t):
                wait(pe, v_done, t + 1)
                for i in range(2):
                    wait(pe, p_lo_done, 2 * t + i + 1)
                    for h in range(HH):
                        for k, part_of_p in enumerate((pT_hi, pT_lo)):
                            mm = nc.tensor.matmul(half_ps[i][:, h * VW:(h + 1) * VW], part_of_p[:, HH * i + h], v_parts[:],
                                                  start=(k == 0), stop=(k == 1))
                    mm.then_inc(ctx_mm, 1)

            def turn_context(t, mid):
                wait(pe, ctx_done, 2 * t + 2)
                if mid:
                    wait(pe, k_ready, t + 2)
                for c in range(C):
                    mm = nc.tensor.transpose(bank_a[:, c * S:(c + 1) * S],
                                             ctx_n[:, HH * c:HH * c + HH].rearrange("p h d -> p (h d)"), ident_sb[:])
                mm.then_inc(c_turned, 1)

            def project_out(t, mid):
                wait(pe, c_lo_done, t + 1)
                if mid:
                    wait(pe, q_ready, t + 2)
                for c in range(C):
                    mm = three_passes(bank_b[:, 0:HID], cT_hi[:, c], cT_lo[:, c], wo_hi[:, c], wo_lo[:, c], c == 0, c == C - 1)
                mm.then_inc(wo_mm, 1)

            def turn_x2(t, s, m):
                wait(pe, x2n_done, t + 1)
                if m is not None:
                    wait(pe, m_done, NPAIR * m + 3 + s)
                for c in range(C):
                    mm = nc.tensor.transpose(mlp_ps[:, 2 * s + 1, 0, c * S:(c + 1) * S], x2n[:, s, c * P:(c + 1) * P], ident_sb[:])
                mm.then_inc(x2_turned, 1)

            def mlp_piece(m, i, turned):
                if i < 2 * J:
                    j, which = divmod(i, 2)
                    q = j // 2
                    if i == 0:
                        wait(pe, h2_lo_done, 2 * m + 2)
                        wait(pe, y_done, 2 * m)
                    elif i % 4 == 0:
                        wait(pe, m_done, NPAIR * m + q - 1)
                    ps = mlp_ps[:, 2 * (q % 2) + j % 2, which]
                    for c in range(C):
                        cols = slice(j * P, (j + 1) * P)
                        mm = three_passes(ps, wgu_hi[:, c, which, cols], wgu_lo[:, c, which, cols],
                                          h2_hi[:, c], h2_lo[:, c], c == 0, c == C - 1)
                    if i % 4 == 3:
                        mm.then_inc(gu_mm, 1)
                else:
                    s, k = ((0, 0), (0, 1), (0, 2), (1, 0), (1, 1), (1, 2), (0, 3), (1, 3))[i - 2 * J]
                    if s == 0 and k == 0:
                        wait(pe, m_done, NPAIR * m + 3)
                    if s == 1 and k == 0 and turned:
                        wait(pe, h2_lo_done, 2 * m + 3)
                    if s == 0:
                        wait(pe, m_lo_done, NPAIR * m + k + 1)
                    for j in (2 * k, 2 * k + 1):
                        tokens = slice(s * S, (s + 1) * S)
                        mm = three_passes(mlp_ps[:, s, 0], m_hi[:, j, tokens], m_lo[:, j, tokens],
                                          wd_hi[:, j], wd_lo[:, j], j == 0, j == J - 1)
                    if k == 3:
                        mm.then_inc(down_mm, 1)

            def part(g, m, more):
                pieces = iter(range(0 if m is None else 24))

                def mlp(n):
                    for _ in range(n):
                        i = next(pieces, None)
                        if i is not None:
                            mlp_piece(m, i, g is not None)

                if g is None:
                    mlp(24)
                    return
                for s in range(2):
                    t = 2 * g + s
                    mid = more or s == 0
                    turn_probs(t, not mid)
                    mlp(2)
                    context(t)
                    mlp(1)
                    if mid:
                        turn_qk(t + 1)
                    mlp(1)
                    turn_context(t, mid)
                    if s == 1:
                        turn_x2(t - 1, 0, m)
                    mlp(1)
                    if mid:
                        scores(t + 1)
                    if m is None and s == 0:
                        pe.wait_ge(o_w_lo, 1)
                    mlp(1)
                    project_out(t, mid)
                    mlp(2)
                    if more:
                        project_qkv(t + 2, s)
                    mlp(1)
                    if s == 1:
                        turn_x2(t, 1, m)
                    mlp(3)
                if m is None:
                    pe.wait_ge(mlp_w_lo, 3)

            pe.wait_ge(ld_cond, 48)
            for n in range(2):
                for c in range(C):
                    for k in range(C):
                        mm = nc.tensor.matmul(half_ps[0][:, (C * n + c) * B:(C * n + c + 1) * B], tw_sb[:, n, k, c * P:(c + 1) * P],
                                              cond_sb[:, k], start=(k == 0), stop=(k == C - 1))
            mm.then_inc(ada_mm, 1)
            pe.wait_ge(qkv_w_lo, 1)
            project_qkv(0, 0)
            pe.wait_ge(ld_ident, 16)
            turn_qk(0)
            scores(0)
            project_qkv(1, 1)
            schedule(pe, part)

        @block.vector
        def _(dve):
            def norm1_low(t, s):
                wait(dve, h_hi_done, t + 1)
                for c in range(C):
                    lo = nc.vector.scalar_tensor_tensor(h_lo[:, s, c], xT_sb[:, pick(t), c].rearrange("p o t -> p (o t)"),
                                                        ada[:, 0, c, pick(t)], h_hi[:, s, c].bitcast(F32), ALU.mult, ALU.subtract)
                lo.then_inc(h_lo_done, 1)

            def rope(t):
                wait(dve, qkv_done, t + 1)
                wait(dve, rope_step, 3 * t)
                nc.vector.tensor_tensor(rope_c[:], qkv[:, 0:NQ + 1], cos_t[:, pick(t)].broadcast_to([P, NQ + 1, HD]),
                                        ALU.mult).then_inc(rope_step, 1)
                for i in range(2):
                    here, there = slice(i * HALF, (i + 1) * HALF), slice((1 - i) * HALF, (2 - i) * HALF)
                    sw = nc.vector.tensor_tensor(rope_s[:, :, here], qkv[:, 0:NQ + 1, there],
                                                 sin_t[:, pick(t), here].broadcast_to([P, NQ + 1, HALF]), ALU.mult)
                sw.then_inc(rope_step, 1)

            def row_max(t, i):
                half = slice(HH * i, HH * i + HH)
                wait(dve, scores_mm, 2 * t + i + 1)
                wait(dve, exp_done, 2 * (t - 1) + i + 1)
                nc.vector.tensor_reduce(smax[:, half], half_ps[i][:].rearrange("p (h t) -> p h t", t=S), AX.X, ALU.max).then_inc(max_done, 1)
                wait(dve, max_done, 2 * t + i + 1)
                nc.vector.tensor_scalar(shift[:, half], smax[:, half], -SCALE, LOG_P, ALU.mult, ALU.add).then_inc(shift_done, 1)

            def p_low(t, i):
                half = slice(HH * i, HH * i + HH)
                wait(dve, p_hi_done, 2 * t + i + 1)
                nc.vector.tensor_tensor(pT_lo[:, half], (bank_b, bank_a)[i][:].rearrange("p (h t) -> p h t", t=S), pT_hi[:, half],
                                        ALU.subtract).then_inc(p_lo_done, 1)

            def normalise(t, i):
                half = slice(HH * i, HH * i + HH)
                heads_ps = half_ps[i][:, 0:HH * VW].rearrange("p (h w) -> p h w", w=VW)
                wait(dve, ctx_mm, 2 * t + i + 1)
                wait(dve, c_turned, t)
                nc.vector.reciprocal(rden[:, half].unsqueeze(2), heads_ps[:, :, 3 * HD:VW]).then_inc(rden_done, 1)
                nc.vector.tensor_reduce(ctx_sum[:, half], heads_ps[:, :, 0:3 * HD].rearrange("p h (k d) -> p h d k", k=3), AX.X,
                                        ALU.add).then_inc(ctx_summed, 1)
                wait(dve, rden_done, 2 * t + i + 1)
                wait(dve, ctx_summed, 2 * t + i + 1)
                nc.vector.tensor_tensor(ctx_n[:, half], ctx_sum[:, half], rden[:, half].unsqueeze(2).broadcast_to([P, HH, HD]),
                                        ALU.mult).then_inc(ctx_done, 1)

            def c_low(t):
                wait(dve, c_hi_done, t + 1)
                nc.vector.tensor_tensor(cT_lo[:], bank_a[:, 0:HID].rearrange("p (c t) -> p c t", t=S), cT_hi[:].bitcast(F32),
                                        ALU.subtract).then_inc(c_lo_done, 1)

            def residual(t):
                wait(dve, wo_mm, t + 1)
                nc.vector.tensor_tensor(x_sb[:, pick(t)], x_sb[:, pick(t)], bank_b[:, 0:HID].unsqueeze(1), ALU.add).then_inc(x2_done, 1)

            def norm2(t, s):
                wait(dve, x2_done, t + 1)
                wait(dve, rstd2_done, t + 1)
                wait(dve, x2_turned, t - 1)
                nc.vector.tensor_scalar(x2n[:, s:s + 1], x_sb[:, pick(t)], rstd2[:, s:s + 1], None, ALU.mult).then_inc(x2n_done, 1)

            def norm2_low(t, s):
                wait(dve, h2_hi_done, t + 1)
                for c in range(C):
                    tokens = slice(s * S, (s + 1) * S)
                    lo = nc.vector.scalar_tensor_tensor(h2_lo[:, c, tokens], mlp_ps[:, 2 * s + 1, 0, c * S:(c + 1) * S],
                                                        ada[:, 1, c, pick(t)], h2_hi[:, c, tokens].bitcast(F32),
                                                        ALU.mult, ALU.subtract)
                lo.then_inc(h2_lo_done, 1)

            def gate_pair(m, q):
                k = 2 * (q % 2)
                wait(dve, tanh_done, NPAIR * m + q + 1)
                wait(dve, m_done, NPAIR * m + q)
                nc.vector.scalar_tensor_tensor(sg[:], th[:], 1.0, mlp_ps[:, k:k + 2, 0], ALU.add, ALU.mult).then_inc(gate_done, 1)
                wait(dve, gate_done, NPAIR * m + q + 1)
                wait(dve, m_lo_done, NPAIR * m + q)
                nc.vector.scalar_tensor_tensor(act_m[:], sg[:], 0.5, mlp_ps[:, k:k + 2, 1], ALU.mult, ALU.mult).then_inc(m_done, 1)

            def finish(m, s):
                t = 2 * m + s
                wait(dve, down_mm, t + 1)
                nc.vector.tensor_tensor(x_sb[:, pick(t)], x_sb[:, pick(t)], mlp_ps[:, s, 0].unsqueeze(1), ALU.add).then_inc(y_done, 1)

            def part(g, m, more):
                if g is None:
                    for q in range(NPAIR):
                        gate_pair(m, q)
                    finish(m, 0)
                    finish(m, 1)
                    return
                for s in range(2):
                    t = 2 * g + s
                    mid = more or s == 0
                    p_low(t, 0)
                    p_low(t, 1)
                    normalise(t, 0)
                    normalise(t, 1)
                    if m is not None and s == 1:
                        gate_pair(m, 2)
                    if more:
                        norm1_low(t + 2, s)
                    if mid:
                        row_max(t + 1, 0)
                    c_low(t)
                    if s == 1:
                        norm2_low(t - 1, 0)
                    if mid:
                        row_max(t + 1, 1)
                    if m is not None:
                        gate_pair(m, 3 * s)
                    residual(t)
                    if more:
                        rope(t + 2)
                    if m is None and s == 1:
                        dve.wait_ge(mlp_w_hi, 3)
                        nc.vector.tensor_tensor(wd_lo[:], wd_sb[:], wd_hi[:].bitcast(F32), ALU.subtract).then_inc(mlp_w_lo, 1)
                    norm2(t, s)
                    if m is not None and s == 0:
                        gate_pair(m, 1)
                    if m is not None and s == 1:
                        finish(m, 0)
                    if s == 1:
                        norm2_low(t, 1)
                    if m is not None and s == 1:
                        finish(m, 1)

            nc.vector.memset(minus_half[:], -0.5).then_inc(consts_set, 1)
            nc.vector.memset(eps[:], EPS).then_inc(consts_set, 1)
            nc.vector.memset(zeros[:], 0.0).then_inc(consts_set, 1)
            dve.wait_ge(ld_wqkv, 16)
            dve.wait_ge(qkv_w_hi, 1)
            nc.vector.tensor_tensor(wqkv_lo[:], wqkv_sb[:], wqkv_hi[:].bitcast(F32), ALU.subtract).then_inc(qkv_w_lo, 1)
            dve.wait_ge(ada_mm, 1)
            dve.wait_ge(ld_cond, 48)
            for n in range(2):
                for c in range(C):
                    a = nc.vector.tensor_scalar(ada[:, n, c], half_ps[0][:, (C * n + c) * B:(C * n + c + 1) * B], 1.0,
                                                lnw_sb[:, n, c:c + 1], ALU.add, ALU.mult)
            a.then_inc(ada_done, 1)
            dve.wait_ge(ada_done, 1)
            norm1_low(0, 0)
            steps = [0]

            def trig(ins):
                steps[0] += 1
                ins.then_inc(trig_step, 1)
                dve.wait_ge(trig_step, steps[0])

            dve.wait_ge(ld_rope, 32)
            trig(nc.vector.tensor_copy(pos_f[:], pos_sb[:]))
            trig(nc.vector.tensor_tensor(ang[:], pos_f[:].unsqueeze(2).broadcast_to([P, B, HALF]),
                                         freq_sb[:].unsqueeze(1).broadcast_to([P, B, HALF]), ALU.mult))
            trig(nc.vector.tensor_scalar(turns[:, 0], ang[:], 1 / TWO_PI, None, ALU.mult))
            trig(nc.vector.tensor_scalar(turns[:, 1], ang[:], 1 / TWO_PI, 0.25, ALU.mult, ALU.add))
            trig(nc.vector.tensor_scalar(turns[:], turns[:], ROUND, ROUND, ALU.add, ALU.subtract))
            trig(nc.vector.tensor_copy(angle[:, 0], ang[:]))
            trig(nc.vector.tensor_copy(angle[:, 1], ang[:]))
            for piece in (PI_A, PI_B, PI_C):
                trig(nc.vector.scalar_tensor_tensor(angle[:], turns[:], -piece, angle[:], ALU.mult, ALU.add))
            trig(nc.vector.tensor_scalar(angle[:, 1], angle[:, 1], np.pi / 2, None, ALU.add))
            trig(nc.vector.tensor_scalar(angle[:], angle[:], PI_MAX, -PI_MAX, ALU.min, ALU.max))
            assert steps[0] == TRIG_STEPS
            norm1_low(1, 1)
            dve.wait_ge(table_done, 1)
            rope(0)
            row_max(0, 0)
            row_max(0, 1)
            dve.wait_ge(ld_wo, 16)
            dve.wait_ge(o_w_hi, 1)
            nc.vector.tensor_tensor(wo_lo[:], wo_sb[:], wo_hi[:].bitcast(F32), ALU.subtract).then_inc(o_w_lo, 1)
            rope(1)
            schedule(dve, part)


def kernel(x, pos_BxS, cond_2048, L0_cond_ln1_w, L0_cond_ln1_tw, L0_cond_ln2_w, L0_cond_ln2_tw, L0_cond_Wq, L0_cond_Wk,
           L0_cond_Wv, L0_cond_Wo, L0_cond_Wg, L0_cond_Wu, L0_cond_Wd):
    import concourse.bacc as _bacc
    from concourse.bass_utils import run_bass_kernel_spmd as _run

    def rows(a):
        a = np.asarray(a)
        return np.ascontiguousarray(np.moveaxis(a.reshape(-1, P, *a.shape[1:]), 0, 1))

    x = np.asarray(x)
    freq = (1.0 / ROPE_BASE ** (np.arange(0, HD, 2, dtype=np.float32) / HD)).astype(np.float32)
    arrays = {
        "x": np.ascontiguousarray(x.transpose(1, 0, 2)),
        "xT": np.ascontiguousarray(x.reshape(B, S, C, P).transpose(3, 0, 2, 1)),
        "pos": np.ascontiguousarray(np.asarray(pos_BxS).T),
        "inv_freq": np.tile(freq, (P, 1)),
        "ident": np.eye(P, dtype=np.float32),
        "condT": rows(np.asarray(cond_2048).T),
        "tw": np.ascontiguousarray(np.stack([rows(np.asarray(w).T) for w in (L0_cond_ln1_tw, L0_cond_ln2_tw)], 1)),
        "ln_w": np.ascontiguousarray(np.stack([rows(w) for w in (L0_cond_ln1_w, L0_cond_ln2_w)], 1)),
        "wqkv": rows(np.concatenate([np.asarray(w) for w in (L0_cond_Wq, L0_cond_Wk, L0_cond_Wv)]).T),
        "wo": rows(np.asarray(L0_cond_Wo).T),
        "wgu": rows(np.stack([np.asarray(w).T for w in (L0_cond_Wg, L0_cond_Wu)], 1)),
        "wd": rows(np.asarray(L0_cond_Wd).T),
    }
    nc = _bacc.Bacc("TRN2", target_bir_lowering=False, num_devices=1)
    args = [nc.dram_tensor(f"in_{n}_dram", a.shape, mybir.dt.from_np(a.dtype), kind="ExternalInput").ap() for n, a in arrays.items()]
    out = nc.dram_tensor("out_dram", (S, B, HID), F32, kind="ExternalOutput").ap()
    layer_kernel(nc, *args, out)
    r = _run(nc, [{f"in_{n}_dram": a for n, a in arrays.items()}], core_ids=[0])
    return np.ascontiguousarray(r.results[0]["out_dram"].transpose(1, 0, 2))
```

```python
from contextlib import ExitStack

import numpy as np

import concourse.bass as bass
from concourse import mybir
from concourse.alu_op_type import AluOpType as ALU

ACT = mybir.ActivationFunctionType
AX = mybir.AxisListType
F32, F32R, I32 = mybir.dt.float32, mybir.dt.float32r, mybir.dt.int32
F16, BF16 = mybir.dt.float16, mybir.dt.bfloat16

P = 128
B, S, HID = 16, 128, 256
NQ, HD, INTER = 8, 32, 1024
HALF = HD // 2
EPS = 1e-6
ROPE_BASE = 10000.0
C = HID // P
QKV = (NQ + 2) * HD
G = B // 2
TOK = 2 * S
J = INTER // P
NPAIR = J // 2
HH = NQ // 2
VW = 3 * HD + 1
SCALE = float(HD) ** -0.5
LOG_P = 12 * float(np.log(2.0))
TWO_PI = 2 * np.pi
PI_A = 6.28125
PI_B = float(np.round((TWO_PI - PI_A) * 2.0**20) / 2.0**20)
PI_C = float(np.float32(TWO_PI - PI_A - PI_B))
FIRST_SEQS, OTHER_SEQS = slice(0, 2), slice(2, B)
TRIG_STEPS = 9
W_VECTOR = ((0,), (1, 2), (3,), (4,), (5,))
W_SCALAR = W_POOL = ((6, 7), (8,), (9, 10), (11,))
PIECE_COUNT = 3 * J
TAIL = 4
SPARE = dict(before_qk=18, before_scores=3, between_halves=6, after_probs=4, after_context=1, after_qk=1, after_turn=1, after_out=3)
PIECES = (((0, 0, 0, 0, 2, 1, 2, 4), (0, 2, 1, 1, 1, 1, 1, 4)), ((1, 1, 1, 1, 0, 2, 2, 5), (0, 2, 1, 1, 1, 1, 1, 4)),
          ((1, 1, 1, 1, 0, 2, 2, 5), (0, 2, 3, 0, 2, 0, 5, 0)))
ROUND = 1.5 * 2.0**23
PI_MAX = float(np.nextafter(np.float32(np.pi), np.float32(0)))


def layer_kernel(nc, x, xT, pos, inv_freq, ident, condT, tw, ln_w, wqkv, wo, wgu, wd, out):
    with ExitStack() as ctx:
        def sb(name, shape, dt=F32):
            return ctx.enter_context(nc.sbuf_tensor(name, shape, dt))

        def bank(name):
            return ctx.enter_context(nc.psum_tensor(name, [P, 512], F32))

        def sem(name):
            return ctx.enter_context(nc.semaphore(name))

        bank_a = bank("bank_a")
        bank_b = bank("bank_b")
        half_ps = [bank("half0_ps"), bank("half1_ps")]
        mlp_ps = ctx.enter_context(nc.psum_tensor("mlp_ps", [P, 4, 2, TOK], F32))

        ident_sb = sb("ident_sb", [P, P])
        pos_sb, pos_f = sb("pos_sb", [P, B], I32), sb("pos_f", [P, B])
        freq_sb = sb("freq_sb", [P, HALF])
        cond_sb = sb("cond_sb", [P, C, B])
        tw_sb = sb("tw_sb", [P, 2, C, HID])
        lnw_sb = sb("lnw_sb", [P, 2, C])
        wqkv_sb, wqkv_hi, wqkv_lo = sb("wqkv_sb", [P, C, QKV]), sb("wqkv_hi", [P, C, QKV], F32R), sb("wqkv_lo", [P, C, QKV], F32R)
        wo_sb, wo_hi, wo_lo = sb("wo_sb", [P, C, HID]), sb("wo_hi", [P, C, HID], F32R), sb("wo_lo", [P, C, HID], F32R)
        wgu_sb, wgu_hi, wgu_lo = sb("wgu_sb", [P, C, 2, INTER]), sb("wgu_hi", [P, C, 2, INTER], F32R), sb("wgu_lo", [P, C, 2, INTER], F32R)
        wd_sb, wd_hi, wd_lo = sb("wd_sb", [P, J, HID]), sb("wd_hi", [P, J, HID], F32R), sb("wd_lo", [P, J, HID], F32R)
        ada = sb("ada", [P, 2, C, B])
        cos_t, sin_t = sb("cos_t", [P, B, HD]), sb("sin_t", [P, B, HD])
        minus_half, eps, zeros = sb("minus_half", [P, 1]), sb("eps", [P, 1]), sb("zeros", [P, HD])
        table_load = sb("table_load", [P, 2])

        x_sb = sb("x_sb", [P, B, HID])
        xT_sb = sb("xT_sb", [P, B, C, S])
        junk1, junk2 = sb("junk1", [P, HID]), sb("junk2", [P, HID])
        ms1, var1, rstd1 = sb("ms1", [P, 2]), sb("var1", [P, 2]), sb("rstd1", [P, 2])
        ms2, var2, rstd2 = sb("ms2", [P, 2]), sb("var2", [P, 2]), sb("rstd2", [P, 2])
        h_hi, h_lo = sb("h_hi", [P, 2, C, S], F32R), sb("h_lo", [P, 2, C, S], F32R)
        qkv = sb("qkv", [P, NQ + 2, HD])
        rope_c, rope_s, roped = sb("rope_c", [P, NQ + 1, HD]), sb("rope_s", [P, NQ + 1, HD]), sb("roped", [P, NQ + 1, HD])
        q_hl = sb("q_hl", [P, NQ, 2, HD], F32R)
        k_hl = sb("k_hl", [P, 2, 4, HD], F32R)
        q_st = sb("q_st", [P, NQ // 2, S], F32R)
        k_bd = sb("k_bd", [P, 2, 2, S], F32R)
        v_parts, v_rest = sb("v_parts", [P, VW], BF16), sb("v_rest", [P, HD])
        smax, shift = sb("smax", [P, NQ]), sb("shift", [P, NQ])
        probs = sb("probs", [P, NQ, S])
        trig = probs[:].rearrange("p h t -> p (h t)").rearrange("p (n i b f) -> p n i b f", n=2, i=2, b=B)
        turns, angle = trig[:, 0], trig[:, 1]
        ang = junk2[:].rearrange("p (b f) -> p b f", f=HALF)
        pT_hi, pT_lo = sb("pT_hi", [P, NQ, S], F16), sb("pT_lo", [P, NQ, S], F16)
        ctx_sum, rden, ctx_n = sb("ctx_sum", [P, NQ, HD]), sb("rden", [P, NQ]), sb("ctx_n", [P, NQ, HD])
        cT_hi, cT_lo = sb("cT_hi", [P, C, S], F32R), sb("cT_lo", [P, C, S], F32R)
        x2n = sb("x2n", [P, 2, HID])
        h2_hi, h2_lo = sb("h2_hi", [P, B, C, S], F32R), sb("h2_lo", [P, B, C, S], F32R)
        spare = wgu_sb[:, 0].rearrange("p n i -> p (n i)").rearrange("p (n j t) -> p n j t", n=4, t=TOK)
        th, sg, act_m = spare[:, 0], spare[:, 1], spare[:, 2:4]
        m_hi, m_lo = sb("m_hi", [P, J, TOK], F32R), sb("m_lo", [P, J, TOK], F32R)

        ld_xT, ld_x, ld_cond, ld_tw2, ld_wqkv, ld_rope, ld_ident = (
            sem(n) for n in ("ld_xT", "ld_x", "ld_cond", "ld_tw2", "ld_wqkv", "ld_rope", "ld_ident"))
        ld_wo, ld_wgu, ld_wd, stored = sem("ld_wo"), sem("ld_wgu"), sem("ld_wd"), sem("stored")
        ada_mm, ada_done, consts_set, zeros_set, trig_step, table_done = (
            sem(n) for n in ("ada_mm", "ada_done", "consts_set", "zeros_set", "trig_step", "table_done"))
        qkv_w_hi, qkv_w_lo, o_w_hi, o_w_lo, w_hi_act, w_hi_dve, w_lo_pool, w_lo_dve = (
            sem(n) for n in ("qkv_w_hi", "qkv_w_lo", "o_w_hi", "o_w_lo", "w_hi_act", "w_hi_dve", "w_lo_pool", "w_lo_dve"))
        sq1_done, var1_done, rstd1_done, h_hi_done, h_lo_done = (
            sem(n) for n in ("sq1_done", "var1_done", "rstd1_done", "h_hi_done", "h_lo_done"))
        qkv_mm, qkv_done, rope_step, v_step, v_done, q_hi_done, k_hi_done, k_lo_done = (
            sem(n) for n in ("qkv_mm", "qkv_done", "rope_step", "v_step", "v_done", "q_hi_done", "k_hi_done", "k_lo_done"))
        k_turned, q_turned, k_ready, q_ready = (sem(n) for n in ("k_turned", "q_turned", "k_ready", "q_ready"))
        scores_mm, max_done, shift_done, exp_done, p_turned, p_hi_done, p_lo_done = (
            sem(n) for n in ("scores_mm", "max_done", "shift_done", "exp_done", "p_turned", "p_hi_done", "p_lo_done"))
        ctx_mm, ctx_summed, rden_done, ctx_done = (sem(n) for n in ("ctx_mm", "ctx_summed", "rden_done", "ctx_done"))
        c_turned, c_hi_done, c_lo_done, wo_mm, x2_done, sq2_done, var2_done, rstd2_done = (
            sem(n) for n in ("c_turned", "c_hi_done", "c_lo_done", "wo_mm", "x2_done", "sq2_done", "var2_done", "rstd2_done"))
        x2n_done, x2_turned, h2_hi_done, h2_lo_done = (sem(n) for n in ("x2n_done", "x2_turned", "h2_hi_done", "h2_lo_done"))
        gu_mm, tanh_done, last_m_lo = sem("gu_mm"), sem("tanh_done"), sem("last_m_lo")
        primed = gate_done, m_done, m_hi_done, m_lo_done, down_mm, y_done = [
            sem(n) for n in ("gate_done", "m_done", "m_hi_done", "m_lo_done", "down_mm", "y_done")]

        block = ctx.enter_context(nc.Block())

        def wait(engine, semaphore, count):
            if semaphore in primed:
                engine.wait_ge(semaphore, count + 1)
            elif not (isinstance(count, int) and count <= 0):
                engine.wait_ge(semaphore, count)

        def pick(t):
            return bass.ds(t, 1)

        def schedule(engine, part):
            part(0, None, None, True)
            part(1, 0, None, True)
            with engine.Fori(2, G - 1) as g:
                part(g, g - 1, g - 2, True)
            part(G - 1, G - 2, G - 3, False)
            part(None, G - 1, G - 2, False)


        def catches_up(s, m, tail):
            return s == 0 and m is not None and tail is None

        halves = [(c, which, slice(i * INTER // 2, (i + 1) * INTER // 2)) for c in range(C) for which in range(2) for i in range(2)]
        mlp_w = [tuple(w[:, c, which, cols] for w in (wgu_sb, wgu_hi, wgu_lo)) for c, which, cols in halves]
        mlp_w += [tuple(w[:, 2 * i:2 * i + 2] for w in (wd_sb, wd_hi, wd_lo)) for i in range(J // 2)]

        @block.sync
        def _(sp):
            def load_group(g):
                sp.dma_start(xT_sb[:, bass.ds(2 * g, 2)], xT[:, bass.ds(2 * g, 2)]).then_inc(ld_xT, 16)
                sp.dma_start(x_sb[:, bass.ds(2 * g, 2)], x[:, bass.ds(2 * g, 2)]).then_inc(ld_x, 16)

            sp.dma_start(cond_sb[:], condT).then_inc(ld_cond, 16)
            sp.dma_start(tw_sb[:, 0], tw[:, 0]).then_inc(ld_cond, 16)
            load_group(0)
            sp.dma_start(tw_sb[:, 1], tw[:, 1]).then_inc(ld_tw2, 16)
            sp.dma_start(ident_sb[:], ident).then_inc(ld_ident, 16)
            sp.wait_ge(ld_xT, 16)
            sp.wait_ge(ld_x, 16)
            load_group(1)
            sp.dma_start(wgu_sb[:], wgu).then_inc(ld_wgu, 16)
            sp.dma_start(wd_sb[:], wd).then_inc(ld_wd, 16)
            with sp.Fori(2, G) as g:
                sp.wait_ge(ld_xT, 16 * g)
                sp.wait_ge(ld_x, 16 * g)
                load_group(g)
            with sp.Fori(0, G - 1) as g:
                wait(sp, y_done, 2 * g + 2)
                sp.dma_start(out[:, bass.ds(2 * g, 2)], x_sb[:, bass.ds(2 * g, 2)]).then_inc(stored, 16)
            for t in (B - 2, B - 1):
                wait(sp, y_done, t + 1)
                sp.dma_start(out[:, t], x_sb[:, t]).then_inc(stored, 16)
            sp.wait_ge(stored, 16 * (G + 1))

        @block.gpsimd
        def _(pool):
            for s in primed:
                pool.sem_inc(s, 1)
            nc.gpsimd.memset(k_bd[:].bitcast(F32), 0.0).then_inc(zeros_set, 1)
            nc.gpsimd.memset(v_parts[:], 1.0)

            def rstd1_of(t, s):
                wait(pool, sq1_done, t + 1)
                wait(pool, qkv_done, t - 1)
                nc.gpsimd.tensor_tensor(var1[:, s:s + 1], ms1[:, s:s + 1], eps[:], ALU.add).then_inc(var1_done, 1)
                wait(pool, var1_done, t + 1)
                nc.gpsimd.tensor_tensor(rstd1[:, s:s + 1], var1[:, s:s + 1], minus_half[:], ALU.pow).then_inc(rstd1_done, 1)

            def split_v(t):
                v = qkv[:, NQ + 1, :]
                wait(pool, qkv_done, t + 1)
                wait(pool, ctx_mm, 2 * t)
                nc.gpsimd.tensor_tensor(v_parts[:, 0:HD], v, zeros[:], ALU.add).then_inc(v_step, 1)
                wait(pool, v_step, 3 * t + 1)
                nc.gpsimd.tensor_tensor(v_rest[:], v, v_parts[:, 0:HD], ALU.subtract).then_inc(v_step, 1)
                wait(pool, v_step, 3 * t + 2)
                nc.gpsimd.tensor_tensor(v_parts[:, HD:2 * HD], v_rest[:], zeros[:], ALU.add).then_inc(v_step, 1)
                wait(pool, v_step, 3 * t + 3)
                nc.gpsimd.tensor_tensor(v_parts[:, 2 * HD:3 * HD], v_rest[:], v_parts[:, HD:2 * HD],
                                        ALU.subtract).then_inc(v_done, 1)

            def rope_sum(t):
                wait(pool, rope_step, 3 * t + 2)
                wait(pool, q_hi_done, t)
                wait(pool, k_hi_done, t)
                nc.gpsimd.tensor_tensor(roped[:], rope_c[:], rope_s[:], ALU.add).then_inc(rope_step, 1)

            def qk_low(t):
                wait(pool, q_hi_done, t + 1)
                nc.gpsimd.tensor_tensor(q_hl[:, :, 1], roped[:, 0:NQ], q_hl[:, :, 0].bitcast(F32), ALU.subtract)
                wait(pool, k_hi_done, t + 1)
                nc.gpsimd.tensor_tensor(k_hl[:, 1], roped[:, NQ:NQ + 1].broadcast_to([P, 4, HD]), k_hl[:, 0].bitcast(F32),
                                        ALU.subtract).then_inc(k_lo_done, 1)

            def rstd2_of(t, s):
                wait(pool, sq2_done, t + 1)
                wait(pool, x2n_done, t - 1)
                nc.gpsimd.tensor_tensor(var2[:, s:s + 1], ms2[:, s:s + 1], eps[:], ALU.add).then_inc(var2_done, 1)
                wait(pool, var2_done, t + 1)
                nc.gpsimd.tensor_tensor(rstd2[:, s:s + 1], var2[:, s:s + 1], minus_half[:], ALU.pow).then_inc(rstd2_done, 1)

            def low_of_pair(m, q):
                wait(pool, m_hi_done, NPAIR * m + q + 1)
                nc.gpsimd.tensor_tensor(m_lo[:, 2 * q:2 * q + 2], act_m[:, q % 2], m_hi[:, 2 * q:2 * q + 2].bitcast(F32),
                                        ALU.subtract).then_inc(m_lo_done, 1)

            def weight_low(pieces):
                for i in pieces:
                    wide, hi, lo = mlp_w[i]
                    pool.wait_ge(w_hi_act, i + 1 - W_SCALAR[0][0])
                    nc.gpsimd.tensor_tensor(lo, wide, hi.bitcast(F32), ALU.subtract).then_inc(w_lo_pool, 1)

            def part(g, m, tail, more):
                if g is None:
                    for q in range(NPAIR - 1):
                        low_of_pair(m, q)
                    return
                for s in range(2):
                    t = 2 * g + s
                    if catches_up(s, m, tail):
                        rstd2_of(t - 1, 1)
                    if more or s == 0:
                        qk_low(t + 1)
                    if m is None:
                        weight_low(W_POOL[2 * s])
                    if m is not None and s == 1:
                        low_of_pair(m, 1)
                    if more:
                        rstd1_of(t + 2, s)
                    if more or s == 0:
                        split_v(t + 1)
                    if m is None:
                        weight_low(W_POOL[2 * s + 1])
                    if m is not None and s == 1:
                        low_of_pair(m, 2)
                    if not (m is None and s == 1):
                        rstd2_of(t, s)
                    if m is not None and s == 0:
                        low_of_pair(m, 0)
                    if more:
                        rope_sum(t + 2)
                    if m is not None and s == 1:
                        low_of_pair(m, 3)

            pool.wait_ge(consts_set, 3)
            rstd1_of(0, 0)
            rstd1_of(1, 1)
            rope_sum(0)
            qk_low(0)
            split_v(0)
            rope_sum(1)
            schedule(pool, part)

        @block.scalar
        def _(act):
            act.dma_start(pos_sb[:], pos).then_inc(ld_rope, 16)
            act.dma_start(freq_sb[:], inv_freq).then_inc(ld_rope, 16)
            act.dma_start(lnw_sb[:], ln_w).then_inc(ld_cond, 16)
            act.dma_start(wqkv_sb[:], wqkv).then_inc(ld_wqkv, 16)
            act.dma_start(wo_sb[:], wo).then_inc(ld_wo, 16)

            def square1(t, s, loaded):
                wait(act, ld_x, 16 * loaded)
                wait(act, sq1_done, t)
                wait(act, rstd1_done, t - 1)
                nc.scalar.activation(junk1[:], x_sb[:, pick(t)], ACT.Square, scale=HID ** -0.5,
                                     accum_out=ms1[:, s:s + 1]).then_inc(sq1_done, 1)

            def norm1_high(t, s, loaded):
                wait(act, ld_xT, 16 * loaded)
                wait(act, ada_done, 1)
                wait(act, qkv_mm, t - 1)
                for c in range(C):
                    hi = nc.scalar.activation(h_hi[:, s, c], xT_sb[:, pick(t), c], ACT.Copy, scale=ada[:, 0, c, pick(t)])
                hi.then_inc(h_hi_done, 1)

            def qkv_out(t, s):
                wait(act, qkv_mm, t + 1)
                wait(act, rstd1_done, t + 1)
                wait(act, rope_step, 3 * t)
                wait(act, v_done, t)
                nc.scalar.activation(qkv[:], bank_a[:, 0:QKV].rearrange("p (h d) -> p h d", d=HD), ACT.Copy,
                                     scale=rstd1[:, s:s + 1]).then_inc(qkv_done, 1)

            def qk_high(t):
                wait(act, rope_step, 3 * t + 3)
                wait(act, q_turned, t)
                nc.scalar.activation(q_hl[:, :, 0], roped[:, 0:NQ], ACT.Copy).then_inc(q_hi_done, 1)
                wait(act, k_turned, t)
                nc.scalar.activation(k_hl[:, 0], roped[:, NQ:NQ + 1].broadcast_to([P, 4, HD]), ACT.Copy).then_inc(k_hi_done, 1)

            def k_out(t):
                wait(act, k_turned, t + 1)
                wait(act, scores_mm, 2 * t)
                for i in range(2):
                    rows = slice(64 * i, 64 * i + 64)
                    k = nc.scalar.activation(k_bd[rows, :, i], bank_a[rows, 0:2 * S].rearrange("p (l t) -> p l t", l=2), ACT.Copy)
                k.then_inc(k_ready, 1)

            def q_out(t):
                wait(act, q_turned, t + 1)
                nc.scalar.activation(q_st[:], bank_b[:].rearrange("p (h t) -> p h t", t=S), ACT.Copy).then_inc(q_ready, 1)

            def exps(t, i):
                wait(act, shift_done, 2 * t + i + 1)
                wait(act, p_turned, 2 * (t - 1) + i + 1)
                for h in range(HH * i, HH * i + HH):
                    e = nc.scalar.activation(probs[:, h], half_ps[i][:, (h % HH) * S:(h % HH + 1) * S], ACT.Exp,
                                             scale=SCALE, bias=shift[:, h:h + 1])
                e.then_inc(exp_done, 1)

            def p_high(t, i):
                wait(act, p_turned, 2 * t + i + 1)
                wait(act, ctx_mm, 2 * (t - 1) + i + 1)
                nc.scalar.activation(pT_hi[:, HH * i:HH * i + HH], (bank_b, bank_a)[i][:].rearrange("p (h t) -> p h t", t=S),
                                     ACT.Copy).then_inc(p_hi_done, 1)

            def c_high(t):
                wait(act, c_turned, t + 1)
                wait(act, wo_mm, t)
                nc.scalar.activation(cT_hi[:], bank_a[:, 0:HID].rearrange("p (c t) -> p c t", t=S), ACT.Copy).then_inc(c_hi_done, 1)

            def square2(t, s):
                wait(act, x2_done, t + 1)
                wait(act, sq2_done, t)
                wait(act, rstd2_done, t - 1)
                nc.scalar.activation(junk2[:], x_sb[:, pick(t)], ACT.Square, scale=HID ** -0.5,
                                     accum_out=ms2[:, s:s + 1]).then_inc(sq2_done, 1)

            def norm2_high(t):
                wait(act, x2_turned, t + 1)
                for c in range(C):
                    hi = nc.scalar.activation(h2_hi[:, pick(t), c], mlp_ps[:, 3, 0, c * S:(c + 1) * S].unsqueeze(1), ACT.Copy,
                                              scale=ada[:, 1, c, pick(t)])
                hi.then_inc(h2_hi_done, 1)

            def weight_high(pieces):
                for i in pieces:
                    wide, hi, lo = mlp_w[i]
                    act.wait_ge(*((ld_wgu, 16) if i < len(halves) else (ld_wd, 16)))
                    nc.scalar.activation(hi, wide, ACT.Copy).then_inc(w_hi_act, 1)

            def tanh_of_pair(m, q):
                wait(act, gu_mm, NPAIR * m + q + 1)
                wait(act, gate_done, NPAIR * m + q)
                k = 2 * (q % 2)
                nc.scalar.activation(th, mlp_ps[:, k:k + 2, 0], ACT.Tanh, scale=0.5).then_inc(tanh_done, 1)

            def high_of_pair(m, q):
                wait(act, m_done, NPAIR * m + q + 1)
                wait(act, down_mm, 2 * m)
                nc.scalar.activation(m_hi[:, 2 * q:2 * q + 2], act_m[:, q % 2], ACT.Copy).then_inc(m_hi_done, 1)

            def part(g, m, tail, more):
                if g is None:
                    norm2_high(B - 1)
                    for q in range(NPAIR):
                        tanh_of_pair(m, q)
                        high_of_pair(m, q)
                    return
                for s in range(2):
                    t = 2 * g + s
                    mid = more or s == 0
                    p_high(t, 0)
                    p_high(t, 1)
                    if catches_up(s, m, tail):
                        square2(t - 1, 1)
                    if mid:
                        qk_high(t + 1)
                    if m is not None:
                        norm2_high(t - 1)
                    if m is not None and s == 1:
                        high_of_pair(m, 1)
                    if more:
                        square1(t + 2, s, g + 2)
                    if m is None:
                        weight_high(W_SCALAR[2 * s])
                    if mid:
                        k_out(t + 1)
                        q_out(t + 1)
                    if m is not None and s == 1:
                        tanh_of_pair(m, 2)
                    c_high(t)
                    if m is None and s == 1:
                        norm2_high(t - 1)
                    if more:
                        norm1_high(t + 2, s, g + 2)
                    if m is None:
                        weight_high(W_SCALAR[2 * s + 1])
                    if m is not None and s == 1:
                        high_of_pair(m, 2)
                    if mid:
                        exps(t + 1, 0)
                    if m is not None and s == 1:
                        tanh_of_pair(m, 3)
                    if not (m is None and s == 1):
                        square2(t, s)
                    if m is not None and s == 0:
                        tanh_of_pair(m, 0)
                    if more:
                        qkv_out(t + 2, s)
                    if mid:
                        exps(t + 1, 1)
                    if m is not None and s == 0:
                        high_of_pair(m, 0)
                        tanh_of_pair(m, 1)
                    if m is not None and s == 1:
                        high_of_pair(m, 3)

            def rope_tables(seqs, steps):
                act.wait_ge(trig_step, steps)
                for i, sign in ((0, -1.0), (1, 1.0)):
                    cols = slice(i * HALF, (i + 1) * HALF)
                    nc.scalar.activation(sin_t[:, seqs, cols], angle[:, 0, seqs], ACT.Sin, scale=sign)
                    table = nc.scalar.activation(cos_t[:, seqs, cols], angle[:, 1, seqs], ACT.Sin)
                table.then_inc(table_done, 1)

            act.wait_ge(consts_set, 3)
            nc.scalar.activation(table_load[:, 0:1], eps[:], ACT.Sin)
            square1(0, 0, 1)
            act.wait_ge(ld_wqkv, 16)
            nc.scalar.activation(wqkv_hi[:], wqkv_sb[:], ACT.Copy).then_inc(qkv_w_hi, 1)
            norm1_high(0, 0, 1)
            rope_tables(FIRST_SEQS, 1 + TRIG_STEPS)
            qkv_out(0, 0)
            square1(1, 1, 1)
            norm1_high(1, 1, 1)
            act.wait_ge(ld_wo, 16)
            nc.scalar.activation(wo_hi[:], wo_sb[:], ACT.Copy).then_inc(o_w_hi, 1)
            qk_high(0)
            rope_tables(OTHER_SEQS, 1 + 2 * TRIG_STEPS)
            act.wait_ge(zeros_set, 1)
            k_out(0)
            q_out(0)
            nc.scalar.activation(table_load[:, 1:2], eps[:], ACT.Exp)
            act.wait_ge(table_done, 2)
            exps(0, 0)
            exps(0, 1)
            qkv_out(1, 1)
            schedule(act, part)

        @block.tensor
        def _(pe):
            def three_passes(out_ap, a_hi, a_lo, b_hi, b_lo, first, last):
                nc.tensor.matmul(out_ap, a_hi, b_hi, start=first, stop=False)
                nc.tensor.matmul(out_ap, a_hi, b_lo, start=False, stop=False)
                return nc.tensor.matmul(out_ap, a_lo, b_hi, start=False, stop=last)

            def keep_warm(n):
                for _ in range(n):
                    nc.tensor.matmul(mlp_ps[:, 0, 0], wqkv_hi[:, 0, 0:P], wqkv_hi[:, 0, 0:TOK], start=True, stop=True)

            def project_qkv(t, s):
                wait(pe, h_lo_done, t + 1)
                wait(pe, c_lo_done, t - 1)
                for c in range(C):
                    mm = three_passes(bank_a[:, 0:QKV], h_hi[:, s, c], h_lo[:, s, c], wqkv_hi[:, c], wqkv_lo[:, c],
                                      c == 0, c == C - 1)
                mm.then_inc(qkv_mm, 1)

            def turn_qk(t):
                wait(pe, k_lo_done, t + 1)
                wait(pe, p_lo_done, 2 * t)
                for i in range(2):
                    mm = nc.tensor.transpose(bank_a[:, i * S:(i + 1) * S],
                                             k_hl[:, i].rearrange("p r d -> p (r d)").bitcast(F32), ident_sb[:])
                mm.then_inc(k_turned, 1)
                for i in range(NQ // 2):
                    mm = nc.tensor.transpose(bank_b[:, i * S:(i + 1) * S],
                                             q_hl[:, 2 * i:2 * i + 2].rearrange("p h l d -> p (h l d)").bitcast(F32),
                                             ident_sb[:])
                mm.then_inc(q_turned, 1)

            def scores(t):
                wait(pe, k_ready, t + 1)
                wait(pe, q_ready, t + 1)
                for i in range(2):
                    wait(pe, ctx_done, 2 * (t - 1) + i + 1)
                    for a in range(2):
                        for l in range(2):
                            mm = nc.tensor.matmul(half_ps[i][:, a * 2 * S:(a + 1) * 2 * S], q_st[:, 2 * i + a],
                                                  k_bd[:, l].rearrange("p h t -> p (h t)"), start=(l == 0), stop=(l == 1))
                    mm.then_inc(scores_mm, 1)

            def turn_probs(t, last, spare):
                for i in range(2):
                    if spare and i == 1:
                        keep_warm(SPARE["between_halves"])
                    wait(pe, exp_done, 2 * t + i + 1)
                    if i == 0:
                        wait(pe, x2_done, t)
                    elif not last:
                        wait(pe, qkv_done, t + 2)
                    for h in range(HH):
                        mm = nc.tensor.transpose((bank_b, bank_a)[i][:, h * S:(h + 1) * S], probs[:, HH * i + h], ident_sb[:])
                    mm.then_inc(p_turned, 1)

            def context(t):
                wait(pe, v_done, t + 1)
                for i in range(2):
                    wait(pe, p_lo_done, 2 * t + i + 1)
                    for h in range(HH):
                        for k, part_of_p in enumerate((pT_hi, pT_lo)):
                            mm = nc.tensor.matmul(half_ps[i][:, h * VW:(h + 1) * VW], part_of_p[:, HH * i + h], v_parts[:],
                                                  start=(k == 0), stop=(k == 1))
                    mm.then_inc(ctx_mm, 1)

            def turn_context(t, mid):
                wait(pe, ctx_done, 2 * t + 2)
                if mid:
                    wait(pe, k_ready, t + 2)
                for c in range(C):
                    mm = nc.tensor.transpose(bank_a[:, c * S:(c + 1) * S],
                                             ctx_n[:, HH * c:HH * c + HH].rearrange("p h d -> p (h d)"), ident_sb[:])
                mm.then_inc(c_turned, 1)

            def project_out(t, mid):
                wait(pe, c_lo_done, t + 1)
                if mid:
                    wait(pe, q_ready, t + 2)
                for c in range(C):
                    mm = three_passes(bank_b[:, 0:HID], cT_hi[:, c], cT_lo[:, c], wo_hi[:, c], wo_lo[:, c], c == 0, c == C - 1)
                mm.then_inc(wo_mm, 1)

            def turn_x2(t, s, pairs):
                wait(pe, x2n_done, t + 1)
                if pairs is not None:
                    wait(pe, m_done, pairs)
                for c in range(C):
                    mm = nc.tensor.transpose(mlp_ps[:, 3, 0, c * S:(c + 1) * S], x2n[:, s, c * P:(c + 1) * P], ident_sb[:])
                mm.then_inc(x2_turned, 1)

            def mlp_piece(m, i, turned):
                if i < 2 * J:
                    j, which = divmod(i, 2)
                    q = j // 2
                    if i == 0 and isinstance(m, int) and m == 0:
                        pe.wait_ge(w_lo_pool, sum(map(len, W_POOL)))
                        pe.wait_ge(w_lo_dve, sum(map(len, W_VECTOR)))
                    if i == 0:
                        wait(pe, h2_lo_done, 2 * m + 2)
                        wait(pe, y_done, 2 * m - 1)
                    elif i == 2:
                        wait(pe, y_done, 2 * m)
                    elif i % 4 == 0:
                        wait(pe, m_done, NPAIR * m + q - 1)
                    if i == 14 and turned:
                        wait(pe, h2_lo_done, 2 * m + 3)
                    ps = mlp_ps[:, 2 * (q % 2) + j % 2, which].rearrange("p (b t) -> p b t", t=S)
                    for c in range(C):
                        cols = slice(j * P, (j + 1) * P)
                        mm = three_passes(ps, wgu_hi[:, c, which, cols], wgu_lo[:, c, which, cols],
                                          h2_hi[:, bass.ds(2 * m, 2), c], h2_lo[:, bass.ds(2 * m, 2), c], c == 0, c == C - 1)
                    if i % 4 == 3:
                        mm.then_inc(gu_mm, 1)
                else:
                    s, k = ((0, 0), (0, 1), (1, 0), (0, 2), (1, 1), (1, 2), (0, 3), (1, 3))[i - 2 * J]
                    if s == 0 and k == 0:
                        wait(pe, m_done, NPAIR * m + 3)
                    if s == 0 and k == 3 and not turned:
                        wait(pe, last_m_lo, 1)
                    elif s == 0:
                        wait(pe, m_lo_done, NPAIR * m + k + 1)
                    for j in (2 * k, 2 * k + 1):
                        tokens = slice(s * S, (s + 1) * S)
                        mm = three_passes(mlp_ps[:, s, 0], m_hi[:, j, tokens], m_lo[:, j, tokens],
                                          wd_hi[:, j], wd_lo[:, j], j == 0, j == J - 1)
                    if k == 3:
                        mm.then_inc(down_mm, 1)

            def part(g, m, tail, more):
                pieces = [(tail, i) for i in range(PIECE_COUNT - TAIL, PIECE_COUNT) if tail is not None and g is not None]
                pieces += [(m, i) for i in range(PIECE_COUNT - TAIL if more else PIECE_COUNT) if m is not None]
                pieces = iter(pieces)
                counts = PIECES[0 if tail is None else 1 if more else 2]

                def mlp(n):
                    for _ in range(n):
                        which = next(pieces, None)
                        if which is not None:
                            mlp_piece(*which, g is not None)

                if g is None:
                    mlp(PIECE_COUNT)
                    return
                for s in range(2):
                    n = iter(counts[s])
                    t = 2 * g + s
                    mid = more or s == 0
                    spare = tail is None and (m is None or s == 0)
                    turn_probs(t, not mid, spare)
                    if spare:
                        keep_warm(SPARE["after_probs"])
                    mlp(next(n))
                    if s == 0 and tail is not None:
                        turn_x2(t - 1, 1, NPAIR * (tail + 1))
                    mlp(next(n))
                    if s == 1 and m is not None:
                        turn_x2(t - 1, 0, NPAIR * m + 2)
                    context(t)
                    if spare:
                        keep_warm(SPARE["after_context"])
                    if catches_up(s, m, tail):
                        turn_x2(t - 1, 1, None)
                    mlp(next(n))
                    if mid:
                        turn_qk(t + 1)
                    if spare:
                        keep_warm(SPARE["after_qk"])
                    mlp(next(n))
                    turn_context(t, mid)
                    if spare and m is None:
                        keep_warm(SPARE["after_turn"])
                    if s == 1 and m is None:
                        turn_x2(t - 1, 0, None)
                    mlp(next(n))
                    if mid:
                        scores(t + 1)
                    if m is None and s == 0:
                        pe.wait_ge(o_w_lo, 1)
                    mlp(next(n))
                    project_out(t, mid)
                    if spare and m is None:
                        keep_warm(SPARE["after_out"])
                    mlp(next(n))
                    if more:
                        project_qkv(t + 2, s)
                    mlp(next(n))
                if not more:
                    turn_x2(B - 1, 1, NPAIR * (m + 1))
                    mlp(PIECE_COUNT)

            pe.wait_ge(ld_cond, 48)
            for n in range(2):
                if n == 1:
                    pe.wait_ge(ld_tw2, 16)
                for c in range(C):
                    for k in range(C):
                        mm = nc.tensor.matmul(half_ps[n][:, c * B:(c + 1) * B], tw_sb[:, n, k, c * P:(c + 1) * P],
                                              cond_sb[:, k], start=(k == 0), stop=(k == C - 1))
                mm.then_inc(ada_mm, 1)
            pe.wait_ge(qkv_w_lo, 1)
            project_qkv(0, 0)
            pe.wait_ge(ld_ident, 16)
            keep_warm(SPARE["before_qk"])
            turn_qk(0)
            keep_warm(SPARE["before_scores"])
            scores(0)
            project_qkv(1, 1)
            schedule(pe, part)

        @block.vector
        def _(dve):
            def norm1_low(t, s):
                wait(dve, h_hi_done, t + 1)
                for c in range(C):
                    lo = nc.vector.scalar_tensor_tensor(h_lo[:, s, c], xT_sb[:, pick(t), c].rearrange("p o t -> p (o t)"),
                                                        ada[:, 0, c, pick(t)], h_hi[:, s, c].bitcast(F32), ALU.mult, ALU.subtract)
                lo.then_inc(h_lo_done, 1)

            def rope(t):
                wait(dve, qkv_done, t + 1)
                wait(dve, rope_step, 3 * t)
                nc.vector.tensor_tensor(rope_c[:], qkv[:, 0:NQ + 1], cos_t[:, pick(t)].broadcast_to([P, NQ + 1, HD]),
                                        ALU.mult).then_inc(rope_step, 1)
                for i in range(2):
                    here, there = slice(i * HALF, (i + 1) * HALF), slice((1 - i) * HALF, (2 - i) * HALF)
                    sw = nc.vector.tensor_tensor(rope_s[:, :, here], qkv[:, 0:NQ + 1, there],
                                                 sin_t[:, pick(t), here].broadcast_to([P, NQ + 1, HALF]), ALU.mult)
                sw.then_inc(rope_step, 1)

            def row_max(t, i):
                half = slice(HH * i, HH * i + HH)
                wait(dve, scores_mm, 2 * t + i + 1)
                wait(dve, exp_done, 2 * (t - 1) + i + 1)
                nc.vector.tensor_reduce(smax[:, half], half_ps[i][:].rearrange("p (h t) -> p h t", t=S), AX.X, ALU.max).then_inc(max_done, 1)
                wait(dve, max_done, 2 * t + i + 1)
                nc.vector.tensor_scalar(shift[:, half], smax[:, half], -SCALE, LOG_P, ALU.mult, ALU.add).then_inc(shift_done, 1)

            def p_low(t, i):
                half = slice(HH * i, HH * i + HH)
                wait(dve, p_hi_done, 2 * t + i + 1)
                nc.vector.tensor_tensor(pT_lo[:, half], (bank_b, bank_a)[i][:].rearrange("p (h t) -> p h t", t=S), pT_hi[:, half],
                                        ALU.subtract).then_inc(p_lo_done, 1)

            def context_sums(t, i):
                half = slice(HH * i, HH * i + HH)
                heads_ps = half_ps[i][:, 0:HH * VW].rearrange("p (h w) -> p h w", w=VW)
                wait(dve, ctx_mm, 2 * t + i + 1)
                nc.vector.reciprocal(rden[:, half].unsqueeze(2), heads_ps[:, :, 3 * HD:VW]).then_inc(rden_done, 1)
                nc.vector.tensor_reduce(ctx_sum[:, half], heads_ps[:, :, 0:3 * HD].rearrange("p h (k d) -> p h d k", k=3), AX.X,
                                        ALU.add).then_inc(ctx_summed, 1)

            def normalise(t, i):
                half = slice(HH * i, HH * i + HH)
                wait(dve, rden_done, 2 * t + i + 1)
                wait(dve, ctx_summed, 2 * t + i + 1)
                wait(dve, c_turned, t)
                nc.vector.tensor_tensor(ctx_n[:, half], ctx_sum[:, half], rden[:, half].unsqueeze(2).broadcast_to([P, HH, HD]),
                                        ALU.mult).then_inc(ctx_done, 1)

            def c_low(t):
                wait(dve, c_hi_done, t + 1)
                nc.vector.tensor_tensor(cT_lo[:], bank_a[:, 0:HID].rearrange("p (c t) -> p c t", t=S), cT_hi[:].bitcast(F32),
                                        ALU.subtract).then_inc(c_lo_done, 1)

            def residual(t):
                wait(dve, wo_mm, t + 1)
                nc.vector.tensor_tensor(x_sb[:, pick(t)], x_sb[:, pick(t)], bank_b[:, 0:HID].unsqueeze(1), ALU.add).then_inc(x2_done, 1)

            def norm2(t, s):
                wait(dve, x2_done, t + 1)
                wait(dve, rstd2_done, t + 1)
                wait(dve, x2_turned, t - 1)
                nc.vector.tensor_scalar(x2n[:, s:s + 1], x_sb[:, pick(t)], rstd2[:, s:s + 1], None, ALU.mult).then_inc(x2n_done, 1)

            def norm2_low(t):
                wait(dve, h2_hi_done, t + 1)
                for c in range(C):
                    lo = nc.vector.scalar_tensor_tensor(h2_lo[:, pick(t), c], mlp_ps[:, 3, 0, c * S:(c + 1) * S].unsqueeze(1),
                                                        ada[:, 1, c, pick(t)], h2_hi[:, pick(t), c].bitcast(F32),
                                                        ALU.mult, ALU.subtract)
                lo.then_inc(h2_lo_done, 1)

            def split_weights(pieces):
                for i in pieces:
                    wide, hi, lo = mlp_w[i]
                    dve.wait_ge(ld_wgu, 16)
                    nc.vector.tensor_copy(hi, wide).then_inc(w_hi_dve, 1)
                for i in pieces:
                    wide, hi, lo = mlp_w[i]
                    dve.wait_ge(w_hi_dve, i + 1)
                    nc.vector.tensor_tensor(lo, wide, hi.bitcast(F32), ALU.subtract).then_inc(w_lo_dve, 1)

            def gate_pair(m, q):
                silu(m, q)
                gated(m, q)

            def silu(m, q):
                k = 2 * (q % 2)
                wait(dve, tanh_done, NPAIR * m + q + 1)
                wait(dve, m_done, NPAIR * m + q)
                nc.vector.scalar_tensor_tensor(sg, th, 1.0, mlp_ps[:, k:k + 2, 0], ALU.add, ALU.mult).then_inc(gate_done, 1)

            def gated(m, q):
                k = 2 * (q % 2)
                wait(dve, gate_done, NPAIR * m + q + 1)
                wait(dve, m_lo_done, NPAIR * m + q - 1)
                nc.vector.scalar_tensor_tensor(act_m[:, q % 2], sg, 0.5, mlp_ps[:, k:k + 2, 1], ALU.mult, ALU.mult).then_inc(m_done, 1)

            def finish(m, s):
                t = 2 * m + s
                wait(dve, down_mm, t + 1)
                nc.vector.tensor_tensor(x_sb[:, pick(t)], x_sb[:, pick(t)], mlp_ps[:, s, 0].unsqueeze(1), ALU.add).then_inc(y_done, 1)

            def part(g, m, tail, more):
                if g is None:
                    norm2_low(B - 1)
                    finish(tail, 0)
                    finish(tail, 1)
                    for q in range(NPAIR):
                        gate_pair(m, q)
                    dve.wait_ge(m_hi_done, 1 + NPAIR * G)
                    nc.vector.tensor_tensor(m_lo[:, J - 2:J], act_m[:, 1], m_hi[:, J - 2:J].bitcast(F32),
                                            ALU.subtract).then_inc(last_m_lo, 1)
                    finish(m, 0)
                    finish(m, 1)
                    return
                for s in range(2):
                    t = 2 * g + s
                    mid = more or s == 0
                    if m is not None and s == 1:
                        gate_pair(m, 1)
                    p_low(t, 0)
                    p_low(t, 1)
                    if catches_up(s, m, tail):
                        norm2(t - 1, 1)
                    context_sums(t, 0)
                    context_sums(t, 1)
                    normalise(t, 0)
                    normalise(t, 1)
                    if m is not None:
                        norm2_low(t - 1)
                    if tail is not None and s == 0:
                        finish(tail, 0)
                        finish(tail, 1)
                    if m is None:
                        split_weights(W_VECTOR[1 + 2 * s])
                    if m is not None and s == 1:
                        silu(m, 2)
                    if not more and s == 1:
                        gated(m, 2)
                    c_low(t)
                    if m is not None and s == 1 and more:
                        gated(m, 2)
                    if m is None:
                        row_max(t + 1, 0)
                    if more:
                        norm1_low(t + 2, s)
                    if m is not None and mid:
                        row_max(t + 1, 0)
                    if mid:
                        row_max(t + 1, 1)
                    if not more and s == 1:
                        silu(m, 3)
                    residual(t)
                    if m is None and s == 1:
                        norm2_low(t - 1)
                    if m is None:
                        split_weights(W_VECTOR[2 + 2 * s])
                    if m is not None and (more or s == 0):
                        gate_pair(m, 3 * s)
                    if more:
                        rope(t + 2)
                    if not more and s == 1:
                        gated(m, 3)
                    if not (m is None and s == 1):
                        norm2(t, s)

            nc.vector.memset(minus_half[:], -0.5).then_inc(consts_set, 1)
            nc.vector.memset(eps[:], EPS).then_inc(consts_set, 1)
            nc.vector.memset(zeros[:], 0.0).then_inc(consts_set, 1)
            steps = [0]

            def step(ins):
                steps[0] += 1
                ins.then_inc(trig_step, 1)
                dve.wait_ge(trig_step, steps[0])

            def rope_angles(seqs):
                n = seqs.stop - seqs.start
                both, a = angle[:, :, seqs], ang[:, seqs]
                step(nc.vector.tensor_tensor(a, pos_f[:, seqs].unsqueeze(2).broadcast_to([P, n, HALF]),
                                             freq_sb[:].unsqueeze(1).broadcast_to([P, n, HALF]), ALU.mult))
                step(nc.vector.tensor_scalar(turns[:, 0, seqs], a, 1 / TWO_PI, None, ALU.mult))
                step(nc.vector.tensor_scalar(turns[:, 1, seqs], a, 1 / TWO_PI, 0.25, ALU.mult, ALU.add))
                step(nc.vector.tensor_scalar(turns[:, :, seqs], turns[:, :, seqs], ROUND, ROUND, ALU.add, ALU.subtract))
                step(nc.vector.scalar_tensor_tensor(both, turns[:, :, seqs], -PI_A, a.unsqueeze(1).broadcast_to([P, 2, n, HALF]), ALU.mult, ALU.add))

            def reduce_angles(seqs):
                both = angle[:, :, seqs]
                step(nc.vector.scalar_tensor_tensor(both, turns[:, :, seqs], -PI_B, both, ALU.mult, ALU.add))
                step(nc.vector.scalar_tensor_tensor(both, turns[:, :, seqs], -PI_C, both, ALU.mult, ALU.add))
                step(nc.vector.tensor_scalar(angle[:, 1, seqs], angle[:, 1, seqs], np.pi / 2, None, ALU.add))
                step(nc.vector.tensor_scalar(both, both, PI_MAX, -PI_MAX, ALU.min, ALU.max))

            def ada_of(n):
                dve.wait_ge(ada_mm, n + 1)
                for c in range(C):
                    a = nc.vector.tensor_scalar(ada[:, n, c], half_ps[n][:, c * B:(c + 1) * B], 1.0,
                                                lnw_sb[:, n, c:c + 1], ALU.add, ALU.mult)
                a.then_inc(ada_done, 1)

            dve.wait_ge(ld_rope, 32)
            step(nc.vector.tensor_copy(pos_f[:], pos_sb[:]))
            rope_angles(FIRST_SEQS)
            reduce_angles(FIRST_SEQS)
            dve.wait_ge(ld_cond, 48)
            ada_of(0)
            dve.wait_ge(ld_wqkv, 16)
            dve.wait_ge(qkv_w_hi, 1)
            nc.vector.tensor_tensor(wqkv_lo[:], wqkv_sb[:], wqkv_hi[:].bitcast(F32), ALU.subtract).then_inc(qkv_w_lo, 1)
            dve.wait_ge(ada_done, 1)
            norm1_low(0, 0)
            ada_of(1)
            rope_angles(OTHER_SEQS)
            dve.wait_ge(table_done, 1)
            rope(0)
            reduce_angles(OTHER_SEQS)
            norm1_low(1, 1)
            row_max(0, 0)
            row_max(0, 1)
            dve.wait_ge(ld_wo, 16)
            dve.wait_ge(o_w_hi, 1)
            nc.vector.tensor_tensor(wo_lo[:], wo_sb[:], wo_hi[:].bitcast(F32), ALU.subtract).then_inc(o_w_lo, 1)
            split_weights(W_VECTOR[0])
            rope(1)
            dve.wait_ge(table_done, 2)
            schedule(dve, part)


def kernel(x, pos_BxS, cond_2048, L0_cond_ln1_w, L0_cond_ln1_tw, L0_cond_ln2_w, L0_cond_ln2_tw, L0_cond_Wq, L0_cond_Wk,
           L0_cond_Wv, L0_cond_Wo, L0_cond_Wg, L0_cond_Wu, L0_cond_Wd):
    import concourse.bacc as _bacc
    from concourse.bass_utils import run_bass_kernel_spmd as _run

    def rows(a):
        a = np.asarray(a)
        return np.ascontiguousarray(np.moveaxis(a.reshape(-1, P, *a.shape[1:]), 0, 1))

    x = np.asarray(x)
    freq = (1.0 / ROPE_BASE ** (np.arange(0, HD, 2, dtype=np.float32) / HD)).astype(np.float32)
    arrays = {
        "x": np.ascontiguousarray(x.transpose(1, 0, 2)),
        "xT": np.ascontiguousarray(x.reshape(B, S, C, P).transpose(3, 0, 2, 1)),
        "pos": np.ascontiguousarray(np.asarray(pos_BxS).T),
        "inv_freq": np.tile(freq, (P, 1)),
        "ident": np.eye(P, dtype=np.float32),
        "condT": rows(np.asarray(cond_2048).T),
        "tw": np.ascontiguousarray(np.stack([rows(np.asarray(w).T) for w in (L0_cond_ln1_tw, L0_cond_ln2_tw)], 1)),
        "ln_w": np.ascontiguousarray(np.stack([rows(w) for w in (L0_cond_ln1_w, L0_cond_ln2_w)], 1)),
        "wqkv": rows(np.concatenate([np.asarray(w) for w in (L0_cond_Wq, L0_cond_Wk, L0_cond_Wv)]).T),
        "wo": rows(np.asarray(L0_cond_Wo).T),
        "wgu": rows(np.stack([np.asarray(w).T for w in (L0_cond_Wg, L0_cond_Wu)], 1)),
        "wd": rows(np.asarray(L0_cond_Wd).T),
    }
    nc = _bacc.Bacc("TRN2", target_bir_lowering=False, num_devices=1)
    args = [nc.dram_tensor(f"in_{n}_dram", a.shape, mybir.dt.from_np(a.dtype), kind="ExternalInput").ap() for n, a in arrays.items()]
    out = nc.dram_tensor("out_dram", (S, B, HID), F32, kind="ExternalOutput").ap()
    layer_kernel(nc, *args, out)
    r = _run(nc, [{f"in_{n}_dram": a for n, a in arrays.items()}], core_ids=[0])
    return np.ascontiguousarray(r.results[0]["out_dram"].transpose(1, 0, 2))
```
